# Optimizing a Trainium2 kernel written in Bass

```python
import numpy as np
import jax
import jax.numpy as jnp

def _softmax(x, axis=-1):
    return jax.nn.softmax(x, axis=axis)

def _gelu(x):
    return jax.nn.gelu(x, approximate=True)

def _silu(x):
    return jax.nn.silu(x)

def _sigmoid(x):
    return jax.nn.sigmoid(x)

def _layernorm(x, axis=-1, eps=1e-05):
    m = jnp.mean(x, axis=axis, keepdims=True)
    v = jnp.var(x, axis=axis, keepdims=True)
    return (x - m) / jnp.sqrt(v + eps)

def _scatter_add(tgt, idx, src, axis=0):
    return tgt.at[idx].add(src)

def _segment_sum(src, seg, n):
    return jax.ops.segment_sum(src, seg, n)
kernel_name = 'mk_prb_d1_jaxref_r4_2d08ed'

def setup_inputs(seed: int=0):
    np.random.seed(seed)
    _w = jnp.asarray

    def _L0_attn_setup():
        import jax, jax.numpy as jnp
        import numpy as np
        D, STATE, CONV = (256, 16, 4)
        B_, L_ = (8, 512)

        def _ssm_forward(x, conv_w, conv_b, Wd, bd, Wb, Wc, log_a, Wg, bg, Wo, bo):
            b, l, d = x.shape
            xt = jnp.transpose(x, (0, 2, 1))
            xc = jax.lax.conv_general_dilated(xt, conv_w, window_strides=(1,), padding=[(CONV - 1, 0)], feature_group_count=d, dimension_numbers=('NCH', 'OIH', 'NCH'))
            xc = jnp.transpose(xc + conv_b[None, :, None], (0, 2, 1))
            xc = jax.nn.silu(xc)
            delta = jax.nn.softplus(jnp.einsum('bld,ed->ble', xc, Wd) + bd)
            Bm = jnp.einsum('bld,nd->bln', xc, Wb)
            Cm = jnp.einsum('bld,nd->bln', xc, Wc)
            A = -jnp.exp(log_a)

            def step(h, inputs):
                dt, bt, ct, xt_ = inputs
                decay = jnp.exp(A[None] * dt[:, :, None])
                inp = dt[:, :, None] * xt_[:, :, None] * bt[:, None, :]
                h = decay * h + inp
                y = jnp.einsum('bdn,bn->bd', h, ct)
                return (h, y)
            h0 = jnp.zeros((b, d, STATE), dtype=x.dtype)
            seq = (jnp.moveaxis(delta, 1, 0), jnp.moveaxis(Bm, 1, 0), jnp.moveaxis(Cm, 1, 0), jnp.moveaxis(xc, 1, 0))
            _, ys = jax.lax.scan(step, h0, seq)
            y = jnp.moveaxis(ys, 0, 1)
            gate = jax.nn.sigmoid(jnp.einsum('bld,ed->ble', x, Wg) + bg)
            return jnp.einsum('bld,ed->ble', y * gate, Wo) + bo
        key = jax.random.key(seed)
        ks = jax.random.split(key, 12)
        s = 0.02
        return {'x': jax.random.normal(ks[0], (B_, L_, D), dtype=jnp.float32), 'conv_w': jax.random.normal(ks[1], (D, 1, CONV), dtype=jnp.float32) * s, 'conv_b': jnp.zeros((D,), dtype=jnp.float32), 'Wd': jax.random.normal(ks[2], (D, D), dtype=jnp.float32) * s, 'bd': jnp.zeros((D,), dtype=jnp.float32), 'Wb': jax.random.normal(ks[3], (STATE, D), dtype=jnp.float32) * s, 'Wc': jax.random.normal(ks[4], (STATE, D), dtype=jnp.float32) * s, 'log_a': jnp.log(jnp.tile(jnp.linspace(1.0, STATE, STATE, dtype=jnp.float32), (D, 1))), 'Wg': jax.random.normal(ks[5], (D, D), dtype=jnp.float32) * s, 'bg': jnp.zeros((D,), dtype=jnp.float32), 'Wo': jax.random.normal(ks[6], (D, D), dtype=jnp.float32) * s, 'bo': jnp.zeros((D,), dtype=jnp.float32)}
    _L0_attn_in = _L0_attn_setup()

    def _L0_ffn_setup():
        import jax, jax.numpy as jnp
        import numpy as np
        INT4_QMAX = 7.0

        def simulate_quantize_int4(w):
            scale = jnp.max(jnp.abs(w)) / INT4_QMAX
            q = jnp.clip(jnp.round(w / scale), -8.0, 7.0)
            return q * scale
        key = jax.random.key(seed)
        k_x, k_w, k_bias, k_a, k_b = jax.random.split(key, 5)
        d_in, features, rank = (256, 256, 16)
        x = jax.random.normal(k_x, (4, 2048, d_in), dtype=jnp.float32)
        kernel = jax.random.normal(k_w, (d_in, features), dtype=jnp.float32)
        bias = jax.random.normal(k_bias, (features,), dtype=jnp.float32)
        a = jax.random.normal(k_a, (d_in, rank), dtype=jnp.float32) * (1.0 / np.sqrt(d_in))
        b = jax.random.normal(k_b, (rank, features), dtype=jnp.float32) * 0.01
        return {'x': x, 'kernel': kernel, 'bias': bias, 'a': a, 'b': b}
    _L0_ffn_in = _L0_ffn_setup()
    _d = {'L0_attn_x': _L0_attn_in['x'], 'L0_attn_conv_w': _L0_attn_in['conv_w'], 'L0_attn_conv_b': _L0_attn_in['conv_b'], 'L0_attn_Wd': _L0_attn_in['Wd'], 'L0_attn_bd': _L0_attn_in['bd'], 'L0_attn_Wb': _L0_attn_in['Wb'], 'L0_attn_Wc': _L0_attn_in['Wc'], 'L0_attn_log_a': _L0_attn_in['log_a'], 'L0_attn_Wg': _L0_attn_in['Wg'], 'L0_attn_bg': _L0_attn_in['bg'], 'L0_attn_Wo': _L0_attn_in['Wo'], 'L0_attn_bo': _L0_attn_in['bo'], 'L0_ffn_kernel': _L0_ffn_in['kernel'], 'L0_ffn_bias': _L0_ffn_in['bias'], 'L0_ffn_a': _L0_ffn_in['a'], 'L0_ffn_b': _L0_ffn_in['b']}
    _x0 = _d['L0_attn_x']
    _d['L0_attn_x'] = jax.random.normal(jax.random.fold_in(jax.random.key(seed), 1), (4, 1024, 256), dtype=_x0.dtype)
    del _x0
    return _d

def reference(L0_attn_x, L0_attn_conv_w, L0_attn_conv_b, L0_attn_Wd, L0_attn_bd, L0_attn_Wb, L0_attn_Wc, L0_attn_log_a, L0_attn_Wg, L0_attn_bg, L0_attn_Wo, L0_attn_bo, L0_ffn_kernel, L0_ffn_bias, L0_ffn_a, L0_ffn_b):

    def _L0_attn_ref(x, conv_w, conv_b, Wd, bd, Wb, Wc, log_a, Wg, bg, Wo, bo):
        import jax, jax.numpy as jnp
        import numpy as np
        D, STATE, CONV = (256, 16, 4)
        B_, L_ = (8, 512)

        def _ssm_forward(x, conv_w, conv_b, Wd, bd, Wb, Wc, log_a, Wg, bg, Wo, bo):
            b, l, d = x.shape
            xt = jnp.transpose(x, (0, 2, 1))
            xc = jax.lax.conv_general_dilated(xt, conv_w, window_strides=(1,), padding=[(CONV - 1, 0)], feature_group_count=d, dimension_numbers=('NCH', 'OIH', 'NCH'))
            xc = jnp.transpose(xc + conv_b[None, :, None], (0, 2, 1))
            xc = jax.nn.silu(xc)
            delta = jax.nn.softplus(jnp.einsum('bld,ed->ble', xc, Wd) + bd)
            Bm = jnp.einsum('bld,nd->bln', xc, Wb)
            Cm = jnp.einsum('bld,nd->bln', xc, Wc)
            A = -jnp.exp(log_a)

            def step(h, inputs):
                dt, bt, ct, xt_ = inputs
                decay = jnp.exp(A[None] * dt[:, :, None])
                inp = dt[:, :, None] * xt_[:, :, None] * bt[:, None, :]
                h = decay * h + inp
                y = jnp.einsum('bdn,bn->bd', h, ct)
                return (h, y)
            h0 = jnp.zeros((b, d, STATE), dtype=x.dtype)
            seq = (jnp.moveaxis(delta, 1, 0), jnp.moveaxis(Bm, 1, 0), jnp.moveaxis(Cm, 1, 0), jnp.moveaxis(xc, 1, 0))
            _, ys = jax.lax.scan(step, h0, seq)
            y = jnp.moveaxis(ys, 0, 1)
            gate = jax.nn.sigmoid(jnp.einsum('bld,ed->ble', x, Wg) + bg)
            return jnp.einsum('bld,ed->ble', y * gate, Wo) + bo
        return _ssm_forward(x, conv_w, conv_b, Wd, bd, Wb, Wc, log_a, Wg, bg, Wo, bo)

    def _L0_ffn_ref(x, kernel, bias, a, b):
        import jax, jax.numpy as jnp
        import numpy as np
        INT4_QMAX = 7.0

        def simulate_quantize_int4(w):
            scale = jnp.max(jnp.abs(w)) / INT4_QMAX
            q = jnp.clip(jnp.round(w / scale), -8.0, 7.0)
            return q * scale
        w = simulate_quantize_int4(kernel)
        y = jnp.einsum('bsd,df->bsf', x, w) + bias
        lora = jnp.einsum('bsr,rf->bsf', jnp.einsum('bsd,dr->bsr', x, a), b)
        return y + lora
    x = L0_attn_x
    xn = _layernorm(x, axis=-1)
    x = x + _L0_attn_ref(xn, L0_attn_conv_w, L0_attn_conv_b, L0_attn_Wd, L0_attn_bd, L0_attn_Wb, L0_attn_Wc, L0_attn_log_a, L0_attn_Wg, L0_attn_bg, L0_attn_Wo, L0_attn_bo) + _L0_ffn_ref(xn, L0_ffn_kernel, L0_ffn_bias, L0_ffn_a, L0_ffn_b)
    return x

_drawn_inputs = setup_inputs


def setup_inputs(seed=0):
    import zlib

    import numpy as np

    out = dict(_drawn_inputs(seed))
    spreads = {'L0_attn_conv_b': (0.0, 0.8),
     'L0_attn_bd': (0.0, 0.8),
     'L0_attn_bg': (0.0, 0.8),
     'L0_attn_bo': (0.0, 0.8)}
    factors = {'L0_attn_conv_w': 8.0,
     'L0_attn_Wd': 8.0,
     'L0_attn_Wb': 8.0,
     'L0_attn_Wc': 8.0,
     'L0_attn_log_a': 8.0,
     'L0_attn_Wg': 8.0,
     'L0_attn_Wo': 8.0,
     'L0_ffn_a': 8.0,
     'L0_ffn_b': 8.0}
    for name, (base, spread) in spreads.items():
        noise = np.random.default_rng([zlib.crc32(name.encode()), seed]).standard_normal(out[name].shape)
        drawn = base * np.exp(spread * noise) if base else spread * noise
        out[name] = jnp.asarray(drawn.astype(out[name].dtype))
    for name, factor in factors.items():
        out[name] = (out[name] * factor).astype(out[name].dtype)
    return out
```

```python
from contextlib import ExitStack

import concourse.bass as bass
from concourse import mybir

ALU = mybir.AluOpType
ACT = mybir.ActivationFunctionType
AX = mybir.AxisListType
F32 = mybir.dt.float32
BF16 = mybir.dt.bfloat16
RMAX = bass.bass_isa.ReduceOp.max

P = 128
ROUND = 12582912.0
SPLIT = 6144.0
QMAX = 7.0
EPS = 1e-5

FRONT_ORDER = [("T", 0, 0), ("T", 0, 1), ("V", 0, 0), ("V", 0, 1), ("Z", 0, 0), ("Z", 0, 1),
               ("T", 1, 0), ("T", 1, 1), ("X", 0, 0), ("V", 1, 0), ("V", 1, 1),
               ("Z", 1, 0), ("Z", 1, 1), ("X", 1, 0)]
FRONT_USES = len(FRONT_ORDER)

STATS_STEP = (0, 2)
T_STEP = (1, 3)
V_STEP = (2, 4)
Z_STEP = (3, 5)
X_STEP = (4, 6)
EXTRAS = {3: [("E", 0)], 5: [("E", 1)], 6: [("E", 2), ("G", 0), ("G", 1)],
          7: [("E", 3), ("G", 2), ("G", 3)]}


def build_layer(nc, x, conv_w, conv_b, Wd, bd, Wb, Wc, log_a, Wg, bg, Wo, bo, kern, bias, a, b_, out):
    NB, L, D = x.shape
    STATE = Wb.shape[0]
    TAPS = conv_w.shape[2]
    RANK = a.shape[1]
    PAD = TAPS - 1
    HALVES = D // P
    BLOCKS = 2 * HALVES
    STEPS = STATE // 2
    TILES = 2 * STEPS
    CH = 512
    CHUNKS = L // CH
    TT = CH // P
    RING = 4
    PARTS = 3
    BCR = 2 * STATE
    assert HALVES == 2 and CHUNKS == 2 and STATE == 16 and BCR == 32

    def front_no(row, kind, k, i):
        return FRONT_USES * row + FRONT_ORDER.index((kind, k, i))

    def extras(step, has_out):
        return [e for e in EXTRAS.get(step, []) if has_out or e[0] == "G"]

    def side_no(row, step, what, has_out):
        n = 0
        for s in range(step):
            n += 2 + len(extras(s, has_out))
        n += ([("C", 0), ("C", 1)] + extras(step, has_out)).index(what)
        per = 2 * STEPS + 8
        return n if not has_out else per * row - 4 + n

    LAST_OUT = (2 * STEPS + 8) * NB - 4

    def tile_no(row, i):
        return TILES * row + i

    with ExitStack() as ctx:
        def sb(name, shape, dt=F32):
            return ctx.enter_context(nc.sbuf_tensor(name, shape, dt))

        def pb(name, shape, dt=F32):
            return ctx.enter_context(nc.psum_tensor(name, shape, dt))

        def sem(name):
            return ctx.enter_context(nc.semaphore(name))

        dt_rep = sb("dt_rep", [P, 2, BLOCKS, L])
        u_rep = sb("u_rep", [P, 2, BLOCKS, L])
        bc_parts = sb("bc_parts", [PARTS * BCR, 2, L], BF16)
        c_sb = sb("c_sb", [P, 2, L])
        xnT_front = sb("xnT_front", [P, HALVES, PAD + L])
        xnT_gate = sb("xnT_gate", [P, HALVES, L])
        xnT_out = sb("xnT_out", [P, HALVES, L])
        decay = sb("decay", [P, 2, 2, L])
        hbuf = sb("hbuf", [P, RING, 2, L])
        yg = sb("yg", [P, HALVES, L])
        xin = sb("xin", [P, TT, D])
        xh = sb("xh", [P, HALVES, CH])
        xc = sb("xc", [P, HALVES, CH])
        sp_log = sb("sp_log", [P, HALVES, CH])
        sp_lin = sb("sp_lin", [P, HALVES, CH])
        bc_rest = sb("bc_rest", [2 * BCR, CH])
        xres = sb("xres", [P, 2, 2, D])
        WdT = sb("WdT", [P, HALVES, D])
        WgT = sb("WgT", [P, HALVES, D])
        WoT = sb("WoT", [P, HALVES, D])
        Wff = sb("Wff", [P, HALVES, D])
        WbcT = sb("WbcT", [P, HALVES, PARTS, BCR])
        taps = sb("taps", [P, HALVES * TAPS, P])
        ident = sb("ident", [P, P])
        sum_n2 = sb("sum_n2", [P, 64])
        pick = sb("pick", [PARTS * BCR, BCR, 64], BF16)
        bias_parts = sb("bias_parts", [P, 2, D], BF16)
        ones = sb("ones", [P, P], BF16)
        a_col = sb("a_col", [P, BLOCKS, STEPS])
        bd_col = sb("bd_col", [P, HALVES])
        bg_col = sb("bg_col", [P, HALVES])
        cb_col = sb("cb_col", [P, HALVES])
        cw_col = sb("cw_col", [P, HALVES, TAPS])
        stats = sb("stats", [P, TT, 6])
        mv = sb("mv", [P, TT, 2])
        var_eps = sb("var_eps", [P, TT])
        neg_mean = sb("neg_mean", [P, TT])
        minus_half = sb("minus_half", [P, TT])
        rstd = sb("rstd", [P, TT])
        nmr = sb("nmr", [P, TT])
        mx = sb("mx", [P, 4])
        scale_hi = sb("scale_hi", [P, 1], BF16)
        scale = sb("scale", [P, 8])

        h0 = hbuf[:, 0].rearrange("p s l -> p (s l)")
        wd_nat = h0[:, 0:512].rearrange("p (h d) -> p h d", h=2)
        wg_nat = h0[:, 512:1024].rearrange("p (h d) -> p h d", h=2)
        wo_nat = h0[:, 1024:1536].rearrange("p (h d) -> p h d", h=2)
        h1 = hbuf[:, 1].rearrange("p s l -> p (s l)")
        wbc_nat = h1[0:BCR, 0:D]
        kern_nat = h1[:, 512:1024]
        quant = h1[:, 1024:1536]
        h2 = hbuf[:, 2].rearrange("p s l -> p (s l)")
        a_nat = h2[:, 0:HALVES * RANK].rearrange("p (h r) -> p h r", h=HALVES)
        b_nat = h2[0:RANK, 512:512 + D]
        aT = h2[0:RANK, 1024:1024 + D]
        la_nat = h2[:, 1536:1536 + BLOCKS * STATE].rearrange("p (k n) -> p k n", k=BLOCKS)
        pick_f = h2[0:PARTS * BCR, 1664:1664 + BCR]
        q_hi = h1[:, 1536:2048]
        h3 = hbuf[:, 3].rearrange("p s l -> p (s l)")
        brow = h3[:, 0:D]
        brow2 = h3[:, D:2 * D]
        b_hi = h3[:, 512:512 + D // 2].bitcast(BF16)
        b_mid = h3[:, 768:768 + D // 2].bitcast(BF16)
        b_rest = h3[:, 1024:1024 + D]
        b_rest2 = h3[:, 1280:1280 + D]
        q_lo = h3[:, 1536:2048]
        q_res = hbuf[:, 0, 1, 512:1024]

        y_ps = pb("y_ps", [P, HALVES, L])
        b_ps = pb("b_ps", [P, L])
        side = pb("side", [P, CH])
        front = pb("front", [P, CH])
        y_bank = y_ps[:].rearrange("p h (c t) -> p (h c) t", t=CH)

        w_loaded = sem("w_loaded")
        ident_made = sem("ident_made")
        pool_memsets = sem("pool_memsets")
        dve_chain = sem("dve_chain")
        absmax_all = sem("absmax_all")
        absmax_own = sem("absmax_own")
        w_transposed = sem("w_transposed")
        w_evicted = sem("w_evicted")
        aT_evicted = sem("aT_evicted")
        ab_made = sem("ab_made")
        a_exp = sem("a_exp")
        dve_setup = sem("dve_setup")
        x_loaded = sem("x_loaded")
        ln_stats = sem("ln_stats")
        ln_link = sem("ln_link")
        rstd_ready = sem("rstd_ready")
        nmr_ready = sem("nmr_ready")
        xn_ready = sem("xn_ready")
        front_filled = sem("front_filled")
        front_drained = sem("front_drained")
        xc_ready = sem("xc_ready")
        sp_abs = sem("sp_abs")
        sp_exp = sem("sp_exp")
        sp_ready = sem("sp_ready")
        dt_ready = sem("dt_ready")
        u_ready = sem("u_ready")
        bc_hi = sem("bc_hi")
        bc_mid = sem("bc_mid")
        bc_ready = sem("bc_ready")
        dt_spread = sem("dt_spread")
        u_spread = sem("u_spread")
        gate_copied = sem("gate_copied")
        out_copied = sem("out_copied")
        b_filled = sem("b_filled")
        side_filled = sem("side_filled")
        side_drained = sem("side_drained")
        decay_ready = sem("decay_ready")
        inp_ready = sem("inp_ready")
        h_ready = sem("h_ready")
        prod_ready = sem("prod_ready")
        summed = sem("summed")
        y_gated = sem("y_gated")
        xres_loaded = [sem(f"xres_loaded{i}") for i in range(2)]
        out_stored = [sem(f"out_stored{i}") for i in range(2)]
        DT_DMAS = 16 * 4 * CHUNKS

        x_chunk = x.rearrange("b (c t p) d -> b c p t d", p=P, c=CHUNKS)
        x_pair = x.rearrange("b (j t p) d -> b j p t d", p=P, t=2)
        out_pair = out.rearrange("b (j t p) d -> b j p t d", p=P, t=2)

        block = ctx.enter_context(nc.Block())

        @block.sync
        def _(sp):
            def load_x(row, k):
                if k == 1:
                    sp.wait_ge(front_filled, front_no(row, "T", 0, 1) + 1)
                elif row > 0:
                    sp.wait_ge(front_filled, front_no(row - 1, "T", 1, 1) + 1)
                sp.dma_start(xin[:], x_chunk[row, k]).then_inc(x_loaded, 16)

            def spread(row, k, par):
                for made, ready, rep, done in ((sp_lin, dt_ready, dt_rep, dt_spread),
                                               (sp_log, u_ready, u_rep, u_spread)):
                    sp.wait_ge(ready, HALVES * (CHUNKS * row + k + 1))
                    for blk in range(2):
                        for n2 in range(2):
                            dst = rep[64 * n2:64 * n2 + 64, par, blk:blk + 3:2, k * CH:(k + 1) * CH]
                            sp.dma_start(dst, made[64 * blk:64 * blk + 64]).then_inc(done, 16)

            def copy_gate(row):
                sp.wait_ge(front_drained, front_no(row, "T", 1, 1) + 1)
                for k in range(CHUNKS):
                    sp.dma_start(xnT_gate[:, :, k * CH:(k + 1) * CH],
                                 xnT_front[:, :, PAD + k * CH:PAD + (k + 1) * CH]).then_inc(gate_copied, 16)

            def load_res(row, j):
                n = 2 * row + j // 2
                if n > 0:
                    sp.wait_ge(out_stored[j % 2], 16 * n)
                sp.dma_start(xres[:, j % 2], x_pair[row, j]).then_inc(xres_loaded[j % 2], 16)

            def store(row, j, n):
                sp.wait_ge(side_drained, n + 1)
                sp.dma_start(out_pair[row, j], xres[:, j % 2]).then_inc(out_stored[j % 2], 16)

            def batch(b, has_front, has_out):
                if has_front:
                    load_x(b + 1, 0)
                if has_out:
                    load_res(b - 1, 0)
                    load_res(b - 1, 1)
                if has_front:
                    load_x(b + 1, 1)
                if has_out:
                    store(b - 1, 0, side_no(b, 3, ("E", 0), True))
                    load_res(b - 1, 2)
                if has_front:
                    spread(b + 1, 0, (b + 1) % 2)
                if has_out:
                    store(b - 1, 1, side_no(b, 5, ("E", 1), True))
                    load_res(b - 1, 3)
                if has_front:
                    spread(b + 1, 1, (b + 1) % 2)
                if has_out:
                    store(b - 1, 2, side_no(b, 6, ("E", 2), True))
                    store(b - 1, 3, side_no(b, 7, ("E", 3), True))
                    sp.wait_ge(side_filled, side_no(b, 7, ("E", 3), True) + 1)
                sp.wait_ge(gate_copied, 32 * (b + 1))
                sp.dma_start(xnT_out[:], xnT_gate[:]).then_inc(out_copied, 16)
                if has_front:
                    sp.wait_ge(side_filled, side_no(b, 7, ("G", 3), has_out) + 1)
                    sp.wait_ge(out_copied, 16 * (b + 1))
                    copy_gate(b + 1)

            load_x(0, 0)
            wd2 = [w.rearrange("(h p) d -> p h d", p=P) for w in (Wd, Wg, Wo)]
            sp.dma_start(wd_nat, wd2[0]).then_inc(w_loaded, 16)
            sp.dma_start(wg_nat, wd2[1]).then_inc(w_loaded, 16)
            sp.dma_start(wo_nat, wd2[2]).then_inc(w_loaded, 16)
            sp.dma_start(wbc_nat[0:STATE, :], Wb).then_inc(w_loaded, 16)
            sp.dma_start(wbc_nat[STATE:BCR, :], Wc).then_inc(w_loaded, 16)
            sp.dma_start(cw_col[:], conv_w.rearrange("(h p) o k -> p h (o k)", p=P)).then_inc(w_loaded, 16)
            for col, vec in ((cb_col, conv_b), (bd_col, bd), (bg_col, bg)):
                sp.dma_start(col[:], vec.rearrange("(h p) -> p h", p=P),
                             allow_slow_non_contiguous=True).then_inc(w_loaded, 16)
            sp.dma_start(kern_nat.rearrange("p (h f) -> p h f", h=HALVES),
                         kern.rearrange("(h p) f -> p h f", p=P)).then_inc(w_loaded, 16)
            sp.dma_start(a_nat, a.rearrange("(h p) r -> p h r", p=P)).then_inc(w_loaded, 16)
            sp.dma_start(b_nat, b_).then_inc(w_loaded, 16)
            for n2 in range(2):
                sp.dma_start(la_nat[64 * n2:64 * n2 + 64],
                             log_a.rearrange("(k p) n -> p k n", p=64)).then_inc(w_loaded, 16)
            sp.dma_start(brow, bo.rearrange("(o d) -> o d", o=1).broadcast_to([P, D])).then_inc(w_loaded, 16)
            sp.dma_start(brow2, bias.rearrange("(o d) -> o d", o=1).broadcast_to([P, D])).then_inc(w_loaded, 16)
            load_x(0, 1)
            spread(0, 0, 0)
            spread(0, 1, 0)
            copy_gate(0)
            for b in range(NB):
                batch(b, b < NB - 1, b > 0)
            for j in range(2):
                load_res(NB - 1, j)
            for j in range(4):
                store(NB - 1, j, LAST_OUT + j)
                if j < 2:
                    load_res(NB - 1, j + 2)
            for s in out_stored:
                sp.wait_ge(s, 16 * 2 * NB)

        W_DMAS = 16

        @block.gpsimd
        def _(pool):
            nc.gpsimd.memset(ident[:], 0.0).then_inc(pool_memsets, 1)
            pool.wait_ge(pool_memsets, 1)
            nc.gpsimd.affine_select(out=ident[:], in_=ident[:], compare_op=ALU.not_equal, fill=1.0, base=0,
                                    pattern=[[-1, P]], channel_multiplier=1).then_inc(ident_made, 1)
            nc.gpsimd.memset(xnT_front[:, :, 0:PAD], 0.0).then_inc(pool_memsets, 1)
            nc.gpsimd.memset(decay[:, :, :, 0:1], 0.0).then_inc(pool_memsets, 1)
            nc.gpsimd.memset(minus_half[:], -0.5).then_inc(pool_memsets, 1)
            pool.wait_ge(pool_memsets, 4)
            pool.wait_ge(absmax_own, 1)
            nc.gpsimd.partition_all_reduce(mx[:, 3:4], mx[:, 2:3], P, RMAX).then_inc(absmax_all, 1)

            def inv_std(row, k):
                c = CHUNKS * row + k
                pool.wait_ge(ln_stats, c + 1)
                if c > 0:
                    pool.wait_ge(xn_ready, c)
                nc.gpsimd.tensor_tensor(rstd[:], var_eps[:], minus_half[:], ALU.pow).then_inc(rstd_ready, 1)
                pool.wait_ge(rstd_ready, c + 1)
                nc.gpsimd.tensor_tensor(nmr[:], neg_mean[:], rstd[:], ALU.mult).then_inc(nmr_ready, 1)

            def delta_and_u(row, k):
                c = CHUNKS * row + k
                for h in range(HALVES):
                    pool.wait_ge(sp_ready, HALVES * c + h + 1)
                    nc.gpsimd.tensor_tensor(sp_lin[:, h], sp_lin[:, h], sp_log[:, h],
                                            ALU.add).then_inc(dt_ready, 1)
                for h in range(HALVES):
                    pool.wait_ge(dt_ready, HALVES * c + h + 1)
                    pool.wait_ge(xc_ready, HALVES * c + h + 1)
                    nc.gpsimd.tensor_tensor(sp_log[:, h], sp_lin[:, h], xc[:, h],
                                            ALU.mult).then_inc(u_ready, 1)

            def times_c(row, m, p, has_out):
                t = tile_no(row, 2 * m + p)
                if p == 0:
                    pool.wait_ge(side_drained, side_no(row, m, ("C", 1), has_out) + 1)
                pool.wait_ge(h_ready, t + 1)
                tile = hbuf[:, (2 * m + p) % RING]
                nc.gpsimd.tensor_tensor(tile, tile, c_sb[:, m % 2].unsqueeze(1).broadcast_to([P, 2, L]),
                                        ALU.mult).then_inc(prod_ready, 1)

            def batch(b, has_front, has_out):
                for m in range(STEPS):
                    for k in range(CHUNKS):
                        if has_front and X_STEP[k] == m:
                            delta_and_u(b + 1, k)
                        if has_front and STATS_STEP[k] == m:
                            inv_std(b + 1, k)
                    for p in range(HALVES):
                        times_c(b, m, p, has_out)

            inv_std(0, 0)
            delta_and_u(0, 0)
            inv_std(0, 1)
            delta_and_u(0, 1)
            for b in range(NB):
                batch(b, b < NB - 1, b > 0)

        @block.scalar
        def _(act):
            def norm(row, k):
                c = CHUNKS * row + k
                act.wait_ge(nmr_ready, c + 1)
                for tt in range(TT):
                    ins = nc.scalar.activation(xin[:, tt], xin[:, tt], ACT.Identity,
                                               bias=nmr[:, tt:tt + 1], scale=rstd[:, tt:tt + 1])
                ins.then_inc(xn_ready, 1)

            def evict_T(row, k):
                for h in range(HALVES):
                    if h == 0 and row > 0:
                        act.wait_ge(gate_copied, 32 * row)
                    act.wait_ge(front_filled, front_no(row, "T", k, h) + 1)
                    nc.scalar.copy(xnT_front[:, h, PAD + k * CH:PAD + (k + 1) * CH],
                                   front[:]).then_inc(front_drained, 1)

            def conv_act(row, k):
                c = CHUNKS * row + k
                if c > 0:
                    act.wait_ge(u_ready, HALVES * c)
                for h in range(HALVES):
                    act.wait_ge(front_filled, front_no(row, "V", k, h) + 1)
                    nc.scalar.activation(xh[:, h], front[:], ACT.Identity, bias=cb_col[:, h:h + 1])
                    nc.scalar.activation(xc[:, h], front[:], ACT.Tanh,
                                         bias=cb_col[:, h:h + 1]).then_inc(front_drained, 1)

            def softplus(row, k):
                c = CHUNKS * row + k
                if c > 0:
                    act.wait_ge(dt_spread, 64 * c)
                    act.wait_ge(u_spread, 64 * c)
                for h in range(HALVES):
                    act.wait_ge(front_filled, front_no(row, "Z", k, h) + 1)
                    nc.scalar.activation(sp_log[:, h], front[:], ACT.Abs,
                                         bias=bd_col[:, h:h + 1]).then_inc(sp_abs, 1)
                    nc.scalar.activation(sp_lin[:, h], front[:], ACT.Relu,
                                         bias=bd_col[:, h:h + 1]).then_inc(front_drained, 1)
                for h in range(HALVES):
                    act.wait_ge(sp_abs, HALVES * c + h + 1)
                    nc.scalar.activation(sp_log[:, h], sp_log[:, h], ACT.Exp, scale=-1.0).then_inc(sp_exp, 1)
                for h in range(HALVES):
                    act.wait_ge(sp_exp, HALVES * c + h + 1)
                    nc.scalar.activation(sp_log[:, h], sp_log[:, h], ACT.Ln, bias=1.0).then_inc(sp_ready, 1)

            def bc_high(row, k, par):
                act.wait_ge(front_filled, front_no(row, "X", k, 0) + 1)
                nc.scalar.copy(bc_parts[:, par, k * CH:(k + 1) * CH], front[0:PARTS * BCR]).then_inc(bc_hi, 1)

            def make_decay(row, par, m, p):
                i = 2 * m + p
                t = tile_no(row, i)
                if i == 0:
                    act.wait_ge(dt_spread, DT_DMAS * (row + 1))
                if t >= 2:
                    act.wait_ge(h_ready, t - 1)
                for blk in range(2):
                    kb = 2 * p + blk
                    ins = nc.scalar.activation(decay[:, i % 2, blk, 1:L], dt_rep[:, par, kb, 1:L], ACT.Exp,
                                               scale=a_col[:, kb, m:m + 1])
                ins.then_inc(decay_ready, 1)

            def copy_c(row, m, c, has_out):
                if c == 0 and tile_no(row, 2 * m) >= 4:
                    act.wait_ge(prod_ready, tile_no(row, 2 * (m - 2) + 1) + 1)
                act.wait_ge(side_filled, side_no(row, m, ("C", c), has_out) + 1)
                nc.scalar.copy(c_sb[:, m % 2, c * CH:(c + 1) * CH], side[:]).then_inc(side_drained, 1)

            def gate(row, g, has_out):
                c, h = divmod(g, 2)
                act.wait_ge(side_filled, side_no(row, 6 + c, ("G", g), has_out) + 1)
                nc.scalar.activation(yg[:, h, c * CH:(c + 1) * CH], side[:], ACT.Tanh, scale=0.5,
                                     bias=bg_col[:, h:h + 1]).then_inc(side_drained, 1)

            def batch(b, has_front, has_out):
                par = b % 2
                for m in range(STEPS):
                    make_decay(b, par, m, 0)
                    copy_c(b, m, 0, has_out)
                    make_decay(b, par, m, 1)
                    copy_c(b, m, 1, has_out)
                    if has_front:
                        for k in range(CHUNKS):
                            if T_STEP[k] == m:
                                norm(b + 1, k)
                        for k in range(CHUNKS):
                            if Z_STEP[k] == m:
                                softplus(b + 1, k)
                            if X_STEP[k] == m:
                                bc_high(b + 1, k, (b + 1) % 2)
                        for k in range(CHUNKS):
                            if T_STEP[k] == m:
                                evict_T(b + 1, k)
                            if V_STEP[k] == m:
                                conv_act(b + 1, k)
                    for kind, g in extras(m, has_out):
                        if kind == "G":
                            gate(b, g, has_out)

            act.wait_ge(w_loaded, 16 * W_DMAS)
            for n2 in range(2):
                src = la_nat[64 * n2:64 * n2 + 64].rearrange("p k (m n) -> p k m n", n=2)[:, :, :, n2]
                ins = nc.scalar.activation(a_col[64 * n2:64 * n2 + 64], src, ACT.Exp)
            ins.then_inc(a_exp, 1)
            act.wait_ge(w_transposed, 1)
            for j, w in enumerate((WdT, WgT)):
                nc.scalar.copy(w[:].rearrange("p h d -> p (h d)"), y_bank[:, j]).then_inc(w_evicted, 1)
            nc.scalar.mul(WoT[:].rearrange("p h d -> p (h d)"), y_bank[:, 2], 0.5).then_inc(w_evicted, 1)
            act.wait_ge(dve_setup, 1)
            norm(0, 0)
            evict_T(0, 0)
            conv_act(0, 0)
            softplus(0, 0)
            norm(0, 1)
            evict_T(0, 1)
            bc_high(0, 0, 0)
            conv_act(0, 1)
            softplus(0, 1)
            bc_high(0, 1, 0)
            for b in range(NB):
                batch(b, b < NB - 1, b > 0)

        @block.vector
        def _(dve):
            chain = [0]

            def link(ins):
                chain[0] += 1
                ins.then_inc(dve_chain, 1)
                dve.wait_ge(dve_chain, chain[0])

            def norm_stats(row, k):
                c = CHUNKS * row + k
                dve.wait_ge(x_loaded, 16 * (c + 1))
                for tt in range(TT):
                    ins = nc.vector.bn_stats(stats[:, tt], xin[:, tt])
                ins.then_inc(ln_link, 1)
                dve.wait_ge(ln_link, 2 * c + 1)
                for tt in range(TT):
                    ins = nc.vector.bn_aggr(mv[:, tt], stats[:, tt])
                ins.then_inc(ln_link, 1)
                dve.wait_ge(ln_link, 2 * c + 2)
                nc.vector.tensor_scalar(var_eps[:], mv[:, :, 1], EPS, None, ALU.add)
                nc.vector.tensor_scalar(neg_mean[:], mv[:, :, 0], -1.0, None, ALU.mult).then_inc(ln_stats, 1)

            def silu(row, k):
                for h in range(HALVES):
                    dve.wait_ge(front_drained, front_no(row, "V", k, h) + 1)
                    nc.vector.scalar_tensor_tensor(out=xc[:, h], in0=xc[:, h], scalar=1.0, in1=xh[:, h],
                                                   op0=ALU.add, op1=ALU.mult).then_inc(xc_ready, 1)

            def bc_split(row, k, par):
                c = CHUNKS * row + k
                cols = slice(k * CH, (k + 1) * CH)
                dve.wait_ge(bc_hi, c + 1)
                nc.vector.tensor_tensor(bc_rest[:], front[0:2 * BCR], bc_parts[0:2 * BCR, par, cols],
                                        ALU.subtract).then_inc(front_drained, 1)
                dve.wait_ge(front_drained, front_no(row, "X", k, 0) + 1)
                nc.vector.tensor_copy(bc_parts[0:2 * BCR, par, cols], bc_rest[:]).then_inc(bc_mid, 1)
                dve.wait_ge(bc_mid, c + 1)
                nc.vector.tensor_tensor(bc_parts[0:BCR, par, cols], bc_rest[0:BCR],
                                        bc_parts[0:BCR, par, cols], ALU.subtract).then_inc(bc_ready, 1)

            def times_b(row, par, m, p):
                i = 2 * m + p
                t = tile_no(row, i)
                if i == 0:
                    dve.wait_ge(u_spread, DT_DMAS * (row + 1))
                if p == 0:
                    dve.wait_ge(b_filled, STEPS * row + m + 1)
                if t >= RING:
                    dve.wait_ge(summed, t - RING + 1)
                nc.vector.tensor_tensor(hbuf[:, i % RING], u_rep[:, par, 2 * p:2 * p + 2],
                                        b_ps[:].unsqueeze(1).broadcast_to([P, 2, L]),
                                        ALU.mult).then_inc(inp_ready, 1)

            def scan(row, m, p):
                i = 2 * m + p
                t = tile_no(row, i)
                dve.wait_ge(inp_ready, t + 1)
                dve.wait_ge(decay_ready, t + 1)
                tile = hbuf[:, i % RING].rearrange("p s l -> p (s l)")
                nc.vector.tensor_tensor_scan(tile, decay[:, i % 2].rearrange("p s l -> p (s l)"), tile, 0.0,
                                             ALU.mult, ALU.add).then_inc(h_ready, 1)

            def gate_y(row, has_out):
                dve.wait_ge(side_drained, side_no(row, 7, ("G", 3), has_out) + 1)
                for h in range(HALVES):
                    dve.wait_ge(summed, TILES * (row + 1) - 1 + h)
                    nc.vector.scalar_tensor_tensor(out=yg[:, h], in0=yg[:, h], scalar=1.0, in1=y_ps[:, h],
                                                   op0=ALU.add, op1=ALU.mult).then_inc(y_gated, 1)

            def add_residual(row, j, filled):
                dve.wait_ge(side_filled, filled)
                dve.wait_ge(xres_loaded[j % 2], 16 * (2 * row + j // 2 + 1))
                io = xres[:, j % 2].rearrange("p t d -> p (t d)")
                nc.vector.tensor_tensor(io, side[:], io, ALU.add).then_inc(side_drained, 1)

            def batch(b, has_front, has_out):
                par = b % 2
                for m in range(STEPS):
                    for p in range(HALVES):
                        times_b(b, par, m, p)
                    if has_front:
                        for k in range(CHUNKS):
                            if V_STEP[k] == m:
                                silu(b + 1, k)
                            if X_STEP[k] == m:
                                bc_split(b + 1, k, (b + 1) % 2)
                            if STATS_STEP[k] == m:
                                norm_stats(b + 1, k)
                    scan(b, m, 0)
                    for kind, j in extras(m, has_out):
                        if kind == "E":
                            add_residual(b - 1, j, side_no(b, m, ("E", j), True) + 1)
                    scan(b, m, 1)
                    if m == 1 and has_out:
                        gate_y(b - 1, b > 1)

            nc.vector.memset(ones[:], 1.0)
            nc.vector.memset(bias_parts[:], 0.0)
            dve.wait_ge(w_loaded, 16 * W_DMAS)
            nc.vector.tensor_reduce(mx[:, 0:1], kern_nat, AX.X, ALU.max)
            nc.vector.tensor_reduce(mx[:, 1:2], kern_nat, AX.X, ALU.min).then_inc(dve_chain, 1)
            chain[0] += 1
            dve.wait_ge(dve_chain, chain[0])
            nc.vector.scalar_tensor_tensor(out=mx[:, 2:3], in0=mx[:, 1:2], scalar=-1.0, in1=mx[:, 0:1],
                                           op0=ALU.mult, op1=ALU.max).then_inc(absmax_own, 1)
            nc.vector.tensor_scalar(cb_col[:], cb_col[:], 0.5, None, ALU.mult)
            nc.vector.tensor_scalar(bg_col[:], bg_col[:], 0.5, None, ALU.mult)
            link(nc.vector.tensor_scalar(cw_col[:], cw_col[:], 0.5, None, ALU.mult))
            dve.wait_ge(a_exp, 1)
            nc.vector.tensor_scalar(a_col[:], a_col[:], -1.0, None, ALU.mult).then_inc(dve_setup, 1)
            norm_stats(0, 0)
            dve.wait_ge(ident_made, 1)
            for h in range(HALVES):
                for k in range(TAPS):
                    n = h * TAPS + k
                    ins = nc.vector.tensor_scalar(taps[:, n], ident[:], cw_col[:, h, k:k + 1], None, ALU.mult)
            ins.then_inc(dve_setup, 1)
            nc.vector.tensor_tensor(sum_n2[:], ident[:, 0:64], ident[:, 64:128], ALU.add)
            link(nc.vector.tensor_tensor(pick_f, ident[0:96, 0:32], ident[0:96, 32:64], ALU.add))
            link(nc.vector.tensor_tensor(pick_f, pick_f, ident[0:96, 64:96], ALU.add))
            nc.vector.tensor_copy(pick[:], pick_f.unsqueeze(2).broadcast_to([PARTS * BCR, BCR, 64]))
            dve.wait_ge(w_transposed, 1)
            for part in range(PARTS):
                ins = nc.vector.tensor_copy(WbcT[:, :, part],
                                            y_bank[:, 3, 0:HALVES * BCR].rearrange("p (h r) -> p h r", h=HALVES))
            ins.then_inc(dve_setup, 1)
            nc.vector.tensor_copy(aT, y_bank[0:RANK, 3, 128:128 + D]).then_inc(aT_evicted, 1)
            silu(0, 0)
            norm_stats(0, 1)
            dve.wait_ge(absmax_all, 1)
            s0, s_hi, s_lo, s_res, s_q, s_inv, ns_hi, ns_lo = (scale[:, i:i + 1] for i in range(8))
            link(nc.vector.tensor_scalar(s0, mx[:, 3:4], 1.0 / QMAX, None, ALU.mult))
            link(nc.vector.tensor_copy(scale_hi[:], s0))
            link(nc.vector.tensor_tensor(s_lo, s0, scale_hi[:], ALU.subtract))
            link(nc.vector.scalar_tensor_tensor(out=s_res, in0=scale_hi[:], scalar=-QMAX, in1=mx[:, 3:4],
                                                op0=ALU.mult, op1=ALU.add))
            link(nc.vector.scalar_tensor_tensor(out=s_res, in0=s_lo, scalar=-QMAX, in1=s_res,
                                                op0=ALU.mult, op1=ALU.add))
            link(nc.vector.scalar_tensor_tensor(out=s_q, in0=s_res, scalar=1.0 / QMAX, in1=s0,
                                                op0=ALU.mult, op1=ALU.add))
            link(nc.vector.reciprocal(s_inv, s_q))
            link(nc.vector.tensor_copy(scale_hi[:], s_q))
            link(nc.vector.tensor_tensor(ns_lo, scale_hi[:], s_q, ALU.subtract))
            link(nc.vector.tensor_scalar(ns_hi, scale_hi[:], -1.0, None, ALU.mult))
            link(nc.vector.tensor_scalar(s_hi, s_q, -1.0, None, ALU.mult))
            link(nc.vector.tensor_scalar(quant, kern_nat, s_inv, None, ALU.mult))
            link(nc.vector.tensor_scalar(q_hi, quant, SPLIT, None, ALU.add))
            link(nc.vector.tensor_scalar(q_hi, q_hi, -SPLIT, None, ALU.add))
            link(nc.vector.tensor_tensor(q_lo, quant, q_hi, ALU.subtract))
            link(nc.vector.scalar_tensor_tensor(out=q_res, in0=q_hi, scalar=ns_hi, in1=kern_nat,
                                                op0=ALU.mult, op1=ALU.add))
            link(nc.vector.scalar_tensor_tensor(out=q_res, in0=q_hi, scalar=ns_lo, in1=q_res,
                                                op0=ALU.mult, op1=ALU.add))
            link(nc.vector.scalar_tensor_tensor(out=q_res, in0=q_lo, scalar=s_hi, in1=q_res,
                                                op0=ALU.mult, op1=ALU.add))
            link(nc.vector.scalar_tensor_tensor(out=quant, in0=q_res, scalar=s_inv, in1=quant,
                                                op0=ALU.mult, op1=ALU.add))
            link(nc.vector.tensor_scalar(quant, quant, ROUND, None, ALU.add))
            link(nc.vector.tensor_scalar(quant, quant, -ROUND, -QMAX - 1.0, ALU.add, ALU.max))
            link(nc.vector.tensor_scalar(quant, quant, QMAX, s_q, ALU.min, ALU.mult))
            dve.wait_ge(ab_made, 1)
            nc.vector.tensor_tensor(Wff[:].rearrange("p h d -> p (h d)"), quant, side[:], ALU.add)
            link(nc.vector.tensor_tensor(brow, brow, brow2, ALU.add))
            link(nc.vector.tensor_copy(b_hi, brow))
            link(nc.vector.tensor_tensor(b_rest, brow, b_hi, ALU.subtract))
            link(nc.vector.tensor_copy(b_mid, b_rest))
            link(nc.vector.tensor_tensor(b_rest2, b_rest, b_mid, ALU.subtract))
            for part, src in enumerate((b_hi, b_mid, b_rest2)):
                r = slice(32 * part, 32 * part + 1)
                ins = nc.vector.tensor_copy(bias_parts[r], src[r].unsqueeze(1).broadcast_to([1, 2, D]))
            ins.then_inc(dve_setup, 1)
            bc_split(0, 0, 0)
            silu(0, 1)
            bc_split(0, 1, 0)
            dve.wait_ge(w_evicted, 3)
            dve.wait_ge(dve_setup, 4)
            for b in range(NB):
                batch(b, b < NB - 1, b > 0)
            gate_y(NB - 1, True)
            for j in range(4):
                add_residual(NB - 1, j, LAST_OUT + j + 1)

        @block.tensor
        def _(pe):
            def front_free(row, kind, k, i):
                n = front_no(row, kind, k, i)
                if n > 0:
                    pe.wait_ge(front_drained, n)

            def transposes(row, k):
                pe.wait_ge(xn_ready, CHUNKS * row + k + 1)
                for h in range(HALVES):
                    front_free(row, "T", k, h)
                    for tt in range(TT):
                        ins = nc.tensor.transpose(front[:, tt * P:(tt + 1) * P], xin[:, tt, h * P:(h + 1) * P],
                                                  ident[:])
                    ins.then_inc(front_filled, 1)

            def conv(row, k):
                for h in range(HALVES):
                    front_free(row, "V", k, h)
                    for j in range(TAPS):
                        ins = nc.tensor.matmul(front[:], taps[:, h * TAPS + j],
                                               xnT_front[:, h, k * CH + j:k * CH + j + CH],
                                               start=(j == 0), stop=(j == TAPS - 1))
                    ins.then_inc(front_filled, 1)

            def delta(row, k):
                pe.wait_ge(xc_ready, HALVES * (CHUNKS * row + k + 1))
                for e in range(HALVES):
                    front_free(row, "Z", k, e)
                    for h in range(HALVES):
                        ins = nc.tensor.matmul(front[:], WdT[:, h, e * P:(e + 1) * P], xc[:, h],
                                               start=(h == 0), stop=(h == HALVES - 1))
                    ins.then_inc(front_filled, 1)

            def proj_bc(row, k):
                front_free(row, "X", k, 0)
                for h in range(HALVES):
                    ins = nc.tensor.matmul(front[0:PARTS * BCR], WbcT[:, h].rearrange("p a r -> p (a r)"),
                                           xc[:, h], start=(h == 0), stop=(h == HALVES - 1))
                ins.then_inc(front_filled, 1)

            def fill_b(row, par, m):
                if m == 0:
                    pe.wait_ge(bc_ready, CHUNKS * (row + 1))
                if row + m > 0:
                    pe.wait_ge(inp_ready, tile_no(row, 2 * m))
                for c in range(CHUNKS):
                    ins = nc.tensor.matmul(b_ps[:, c * CH:(c + 1) * CH],
                                           pick[:, 2 * m:2 * m + 2].rearrange("r a q -> r (a q)"),
                                           bc_parts[:, par, c * CH:(c + 1) * CH], start=True, stop=True)
                ins.then_inc(b_filled, 1)

            def side_free(n):
                if n > 0:
                    pe.wait_ge(side_drained, n)

            def fill_c(row, par, m, c, has_out):
                side_free(side_no(row, m, ("C", c), has_out))
                nc.tensor.matmul(side[:], pick[:, STATE + 2 * m:STATE + 2 * m + 2].rearrange("r a q -> r (a q)"),
                                 bc_parts[:, par, c * CH:(c + 1) * CH],
                                 start=True, stop=True).then_inc(side_filled, 1)

            def sum_states(row, i):
                m, p = divmod(i, 2)
                if i == 0 and row > 0:
                    pe.wait_ge(y_gated, HALVES * row)
                pe.wait_ge(prod_ready, tile_no(row, i) + 1)
                for c in range(CHUNKS):
                    for blk in range(2):
                        ins = nc.tensor.matmul(y_ps[64 * blk:64 * blk + 64, p, c * CH:(c + 1) * CH], sum_n2[:],
                                               hbuf[:, i % RING, blk, c * CH:(c + 1) * CH],
                                               start=(m == 0), stop=(m == STEPS - 1))
                ins.then_inc(summed, 1)

            def out_product(row, j, n):
                if j == 0:
                    pe.wait_ge(y_gated, HALVES * (row + 1))
                    pe.wait_ge(out_copied, 16 * (row + 1))
                side_free(n)
                nc.tensor.matmul(side[:], ones[:], bias_parts[:].rearrange("p t d -> p (t d)"),
                                 start=True, stop=False)
                for tt in range(2):
                    tok = slice((2 * j + tt) * P, (2 * j + tt + 1) * P)
                    for src, w in ((xnT_out, Wff), (yg, WoT)):
                        for h in range(HALVES):
                            ins = nc.tensor.matmul(side[:, tt * D:(tt + 1) * D], src[:, h, tok], w[:, h],
                                                   start=False, stop=(tt == 1 and w is WoT and h == HALVES - 1))
                ins.then_inc(side_filled, 1)

            def gate(row, g, has_out):
                c, e = divmod(g, 2)
                if g == 0:
                    pe.wait_ge(gate_copied, 32 * (row + 1))
                side_free(side_no(row, 6 + c, ("G", g), has_out))
                for h in range(HALVES):
                    ins = nc.tensor.matmul(side[:], WgT[:, h, e * P:(e + 1) * P],
                                           xnT_gate[:, h, c * CH:(c + 1) * CH],
                                           start=(h == 0), stop=(h == HALVES - 1))
                ins.then_inc(side_filled, 1)

            def batch(b, has_front, has_out):
                par = b % 2
                for m in range(STEPS):
                    fill_b(b, par, m)
                    for c in range(CHUNKS):
                        fill_c(b, par, m, c, has_out)
                    for i in (2 * m - 4, 2 * m - 3):
                        if i >= 0:
                            sum_states(b, i)
                        elif has_out:
                            sum_states(b - 1, i + TILES)
                    if has_front:
                        for k in range(CHUNKS):
                            if Z_STEP[k] == m:
                                delta(b + 1, k)
                            if X_STEP[k] == m:
                                proj_bc(b + 1, k)
                        for k in range(CHUNKS):
                            if T_STEP[k] == m:
                                transposes(b + 1, k)
                            if V_STEP[k] == m:
                                conv(b + 1, k)
                    for kind, n in extras(m, has_out):
                        if kind == "E":
                            out_product(b - 1, n, side_no(b, m, ("E", n), True))
                        else:
                            gate(b, n, has_out)

            pe.wait_ge(w_loaded, 16 * W_DMAS)
            pe.wait_ge(ident_made, 1)
            for j, nat in enumerate((wd_nat, wg_nat, wo_nat)):
                for h in range(HALVES):
                    for e in range(HALVES):
                        nc.tensor.transpose(y_bank[:, j, h * D + e * P:h * D + (e + 1) * P],
                                            nat[:, e, h * P:(h + 1) * P], ident[:])
            for h in range(HALVES):
                nc.tensor.transpose(y_bank[:, 3, h * BCR:(h + 1) * BCR], wbc_nat[:, h * P:(h + 1) * P],
                                    ident[0:BCR, 0:BCR])
            for h in range(HALVES):
                ins = nc.tensor.transpose(y_bank[0:RANK, 3, 128 + h * P:128 + (h + 1) * P], a_nat[:, h],
                                          ident[:])
            ins.then_inc(w_transposed, 1)
            transposes(0, 0)
            pe.wait_ge(aT_evicted, 1)
            for h in range(HALVES):
                ins = nc.tensor.matmul(side[:, h * D:(h + 1) * D], aT[:, h * P:(h + 1) * P], b_nat,
                                       start=True, stop=True)
            ins.then_inc(ab_made, 1)
            pe.wait_ge(pool_memsets, 3)
            pe.wait_ge(dve_setup, 3)
            conv(0, 0)
            pe.wait_ge(w_evicted, 3)
            delta(0, 0)
            transposes(0, 1)
            proj_bc(0, 0)
            conv(0, 1)
            delta(0, 1)
            proj_bc(0, 1)
            pe.wait_ge(dve_setup, 4)
            for b in range(NB):
                batch(b, b < NB - 1, b > 0)
            for i in range(TILES - 4, TILES):
                sum_states(NB - 1, i)
            for j in range(4):
                out_product(NB - 1, j, LAST_OUT + j)


_INS = ['L0_attn_x', 'L0_attn_conv_w', 'L0_attn_conv_b', 'L0_attn_Wd', 'L0_attn_bd', 'L0_attn_Wb', 'L0_attn_Wc',
        'L0_attn_log_a', 'L0_attn_Wg', 'L0_attn_bg', 'L0_attn_Wo', 'L0_attn_bo', 'L0_ffn_kernel', 'L0_ffn_bias',
        'L0_ffn_a', 'L0_ffn_b']


def kernel(**inputs):
    import numpy as _np
    import concourse.bacc as _bacc
    from concourse import mybir as _mybir
    from concourse.bass_utils import run_bass_kernel_spmd as _run

    nc = _bacc.Bacc("TRN2", target_bir_lowering=False, num_devices=1)
    arrays, args = {}, []
    for name in _INS:
        v = _np.ascontiguousarray(inputs[name])
        arrays[f"in_{name}_dram"] = v
        args.append(nc.dram_tensor(f"in_{name}_dram", v.shape, _mybir.dt.from_np(v.dtype), kind="ExternalInput").ap())
    shape = inputs['L0_attn_x'].shape
    args.append(nc.dram_tensor("out_0_dram", shape, _mybir.dt.float32, kind="ExternalOutput").ap())
    build_layer(nc, *args)
    r = _run(nc, [arrays], core_ids=[0])
    return r.results[0]["out_0_dram"]
```

```python
from contextlib import ExitStack

import concourse.bass as bass
from concourse import mybir

ALU = mybir.AluOpType
ACT = mybir.ActivationFunctionType
AX = mybir.AxisListType
F32 = mybir.dt.float32
BF16 = mybir.dt.bfloat16
RMAX = bass.bass_isa.ReduceOp.max

P = 128
Q = 32
ROUND = 12582912.0
SPLIT = 6144.0
QMAX = 7.0
EPS = 1e-5
TILES = 8

FRONT_SLOTS = {0: [("Z", 0), ("Z", 1)], 1: [("X", 0)], 2: [("T", 0), ("T", 1)], 3: [("V", 0)], 4: [("V", 1)]}
SIDE_SLOTS = {0: [("G", 0), ("G", 1)], 1: [("C", 1)], 3: [("C", 2)], 4: [("E", 0)], 5: [("C", 3)],
              6: [("E", 1)], 7: [("C", 4)]}


def build_layer(nc, x, conv_w, conv_b, Wd, bd, Wb, Wc, log_a, Wg, bg, Wo, bo, kern, bias, a, b_, out):
    NB, L, D = x.shape
    STATE = Wb.shape[0]
    TAPS = conv_w.shape[2]
    RANK = a.shape[1]
    PAD = TAPS - 1
    HALVES = D // P
    NQ = P // Q
    BLOCKS = HALVES * NQ
    QUADS = STATE // NQ
    CH = 512
    ROW_CHUNKS = L // CH
    NC = NB * ROW_CHUNKS
    TT = CH // P
    SEG = CH + 1
    RING = 5
    XRING = 4
    PARTS = 3
    BCR = 2 * STATE
    OUTS = TT // 2
    assert HALVES == 2 and QUADS * HALVES == TILES and BCR == 32 and ROW_CHUNKS == 2

    front_uses = [("T", 0, h) for h in range(HALVES)] + [("V", 0, h) for h in range(HALVES)]
    front_uses += [("T", 1, 0), ("T", 1, 1), ("Z", 0, 0), ("Z", 0, 1), ("X", 0, 0), ("V", 1, 0), ("V", 1, 1)]
    side_uses = [("ab", 0, 0), ("C", 0, 0)]
    for c in range(NC):
        for slot in range(TILES):
            front_uses += [(kind, c + (2 if kind in "TV" else 1), i) for kind, i in FRONT_SLOTS.get(slot, [])
                           if c + (2 if kind in "TV" else 1) < NC]
            for kind, i in SIDE_SLOTS.get(slot, []):
                if kind == "C" and 4 * c + i < 4 * NC:
                    side_uses.append(("C", c + i // 4, i % 4))
                elif kind in "GE" and c > 0:
                    side_uses.append((kind, c - 1, i))
    side_uses += [("G", NC - 1, 0), ("G", NC - 1, 1), ("E", NC - 1, 0), ("E", NC - 1, 1)]

    def front_use(kind, c, i):
        return divmod(front_uses.index((kind, c, i)), 2)[::-1]

    def side_use(kind, c, i):
        return divmod(side_uses.index((kind, c, i)), 2)[::-1]

    with ExitStack() as ctx:
        def sb(name, shape, dt=F32):
            return ctx.enter_context(nc.sbuf_tensor(name, shape, dt))

        def pb(name, shape, dt=F32):
            return ctx.enter_context(nc.psum_tensor(name, shape, dt))

        def sem(name):
            return ctx.enter_context(nc.semaphore(name))

        dt_rep = sb("dt_rep", [P, 2, BLOCKS, CH])
        u_rep = sb("u_rep", [P, 2, BLOCKS, CH])
        bc_parts = sb("bc_parts", [PARTS * BCR, 2, CH], BF16)
        c_sb = sb("c_sb", [P, QUADS, CH])
        xnT = sb("xnT", [P, XRING, HALVES, PAD + CH])
        decay = sb("decay", [P, 2, NQ, SEG])
        hbuf = sb("hbuf", [P, RING, NQ, SEG])
        h_state = sb("h_state", [P, QUADS, HALVES, NQ])
        yg = sb("yg", [P, HALVES, CH])
        xin = sb("xin", [P, 2, TT, D])
        xh = sb("xh", [P, HALVES, CH])
        xc = sb("xc", [P, 2, HALVES, CH])
        sp_log = sb("sp_log", [P, HALVES, CH])
        sp_lin = sb("sp_lin", [P, HALVES, CH])
        bc_rest = sb("bc_rest", [2 * BCR, CH])
        xres = sb("xres", [P, OUTS, 2, D])
        WdT = sb("WdT", [P, HALVES, D])
        WgT = sb("WgT", [P, HALVES, D])
        WoT = sb("WoT", [P, HALVES, D])
        Wff = sb("Wff", [P, HALVES, D])
        WbcT = sb("WbcT", [P, HALVES, PARTS, BCR])
        taps = sb("taps", [P, HALVES * TAPS, P])
        ident = sb("ident", [P, P])
        sum_n4 = sb("sum_n4", [P, Q])
        pick = sb("pick", [PARTS * BCR, BCR, Q], BF16)
        bias_parts = sb("bias_parts", [P, 2, D], BF16)
        ones = sb("ones", [P, P], BF16)
        a_col = sb("a_col", [P, BLOCKS, QUADS])
        bd_col = sb("bd_col", [P, HALVES])
        bg_col = sb("bg_col", [P, HALVES])
        cb_col = sb("cb_col", [P, HALVES])
        cw_col = sb("cw_col", [P, HALVES, TAPS])
        stats = sb("stats", [P, TT, 6])
        mv = sb("mv", [P, TT, 2])
        var_eps = sb("var_eps", [P, TT])
        neg_mean = sb("neg_mean", [P, TT])
        minus_half = sb("minus_half", [P, TT])
        rstd = sb("rstd", [P, TT])
        nmr = sb("nmr", [P, TT])
        mx = sb("mx", [P, 4])
        scale_hi = sb("scale_hi", [P, 1], BF16)
        scale = sb("scale", [P, 8])

        room = u_rep[:, 1].rearrange("p b t -> p (b t)")
        wd_nat = room[:, 0:512].rearrange("p (h d) -> p h d", h=2)
        wg_nat = room[:, 512:1024].rearrange("p (h d) -> p h d", h=2)
        wo_nat = room[:, 1024:1536].rearrange("p (h d) -> p h d", h=2)
        kern_nat = room[:, 1536:2048]
        quant = room[:, 2048:2560]
        q_hi = room[:, 2560:3072]
        q_lo = room[:, 3072:3584]
        q_res = room[:, 3584:4096]
        room2 = dt_rep[:, 1].rearrange("p b t -> p (b t)")
        wbc_nat = room2[0:BCR, 0:D]
        a_nat = room2[:, 256:256 + HALVES * RANK].rearrange("p (h r) -> p h r", h=HALVES)
        b_nat = room2[0:RANK, 512:512 + D]
        aT = room2[0:RANK, 768:768 + D]
        la_nat = room2[:, 1024:1024 + BLOCKS * STATE].rearrange("p (k n) -> p k n", k=BLOCKS)
        pick_f = room2[0:PARTS * BCR, 1152:1152 + BCR]
        brow = room2[:, 1280:1536]
        brow2 = room2[:, 1536:1792]
        b_hi = room2[:, 1792:1920].bitcast(BF16)
        b_mid = room2[:, 1920:2048].bitcast(BF16)
        b_rest = room2[:, 2048:2304]
        b_rest2 = room2[:, 2304:2560]
        spread_q = room2[:, 2560:2560 + NQ * P].rearrange("p (q n d) -> p q n d", q=NQ, n=NQ)

        y_ps = pb("y_ps", [P, HALVES, CH])
        b_ps = pb("b_ps", [P, 2, CH])
        side = pb("side", [P, 2, CH])
        front = pb("front", [P, 2, CH])

        cols_loaded = sem("cols_loaded")
        kern_loaded = sem("kern_loaded")
        wd_loaded = sem("wd_loaded")
        w_loaded = sem("w_loaded")
        ident_made = sem("ident_made")
        pool_memsets = sem("pool_memsets")
        dve_chain = sem("dve_chain")
        absmax_all = sem("absmax_all")
        absmax_own = sem("absmax_own")
        wd_transposed = sem("wd_transposed")
        bca_transposed = sem("bca_transposed")
        w_transposed = sem("w_transposed")
        w_evicted = sem("w_evicted")
        wbc_evicted = sem("wbc_evicted")
        aT_evicted = sem("aT_evicted")
        a_exp = sem("a_exp")
        a_ready = sem("a_ready")
        cols_halved = sem("cols_halved")
        taps_made = sem("taps_made")
        picks_made = sem("picks_made")
        bias_made = sem("bias_made")
        u0_filled = sem("u0_filled")
        u0_copied = [sem(f"u0_copied{i}") for i in range(2)]
        x_loaded = [sem(f"x_loaded{i}") for i in range(2)]
        ln_stats = sem("ln_stats")
        ln_link = sem("ln_link")
        rstd_ready = sem("rstd_ready")
        nmr_ready = sem("nmr_ready")
        xn_ready = sem("xn_ready")
        pad_ready = sem("pad_ready")
        front_filled = [sem(f"front_filled{i}") for i in range(2)]
        front_drained = [sem(f"front_drained{i}") for i in range(2)]
        xc_ready = sem("xc_ready")
        sp_abs = sem("sp_abs")
        sp_exp = sem("sp_exp")
        sp_ready = sem("sp_ready")
        dt_ready = sem("dt_ready")
        u_ready = sem("u_ready")
        bc_hi = sem("bc_hi")
        bc_mid = sem("bc_mid")
        bc_ready = sem("bc_ready")
        dt_spread = sem("dt_spread")
        u_spread = sem("u_spread")
        b_filled = sem("b_filled")
        side_filled = [sem(f"side_filled{i}") for i in range(2)]
        side_drained = [sem(f"side_drained{i}") for i in range(2)]
        decay_ready = sem("decay_ready")
        inp_ready = sem("inp_ready")
        scanned = sem("scanned")
        h_ready = sem("h_ready")
        prod_ready = sem("prod_ready")
        summed = sem("summed")
        y_gated = sem("y_gated")
        xres_loaded = [sem(f"xres_loaded{i}") for i in range(OUTS)]
        out_stored = [sem(f"out_stored{i}") for i in range(OUTS)]
        SPREAD = 16 * NQ * NQ
        COLS = 4
        W_DMAS = 12

        x_chunk = x.rearrange("b (c t p) d -> (b c) p t d", p=P, c=ROW_CHUNKS)
        x_pair = x.rearrange("b (j t p) d -> (b j) p t d", p=P, t=2)
        out_pair = out.rearrange("b (j t p) d -> (b j) p t d", p=P, t=2)

        def wait_filled(eng, sems, use):
            bank, n = use
            eng.wait_ge(sems[bank], n + 1)

        def wait_free(eng, sems, use):
            bank, n = use
            if n > 0:
                eng.wait_ge(sems[bank], n)

        block = ctx.enter_context(nc.Block())

        @block.sync
        def _(sp):
            def load_x(c):
                if c >= 2:
                    wait_filled(sp, front_filled, front_use("T", c - 2, 1))
                sp.dma_start(xin[:, c % 2], x_chunk[c]).then_inc(x_loaded[c % 2], 16)

            def spread(c):
                for made, ready, rep, done in ((sp_lin, dt_ready, dt_rep, dt_spread),
                                               (sp_log, u_ready, u_rep, u_spread))[:2 if c > 0 else 1]:
                    sp.wait_ge(ready, HALVES * (c + 1))
                    for q in range(NQ):
                        for n4 in range(NQ):
                            dst = rep[Q * n4:Q * n4 + Q, c % 2, q:q + NQ + 1:NQ]
                            sp.dma_start(dst, made[Q * q:Q * q + Q]).then_inc(done, 16)

            def load_res(c, j):
                if c > 0:
                    sp.wait_ge(out_stored[j], 16 * c)
                sp.dma_start(xres[:, j], x_pair[OUTS * c + j]).then_inc(xres_loaded[j], 16)

            def store(c, j):
                bank, n = side_use("E", c, j)
                sp.wait_ge(side_drained[bank], n + 1)
                sp.dma_start(out_pair[OUTS * c + j], xres[:, j]).then_inc(out_stored[j], 16)

            load_x(0)
            sp.dma_start(cw_col[:], conv_w.rearrange("(h p) o k -> p h (o k)", p=P)).then_inc(cols_loaded, 16)
            for col, vec in ((cb_col, conv_b), (bd_col, bd), (bg_col, bg)):
                sp.dma_start(col[:], vec.rearrange("(h p) -> p h", p=P),
                             allow_slow_non_contiguous=True).then_inc(cols_loaded, 16)
            sp.dma_start(kern_nat.rearrange("p (h f) -> p h f", h=HALVES),
                         kern.rearrange("(h p) f -> p h f", p=P)).then_inc(kern_loaded, 16)
            load_x(1)
            sp.dma_start(wd_nat, Wd.rearrange("(h p) d -> p h d", p=P)).then_inc(wd_loaded, 16)
            sp.dma_start(wbc_nat[0:STATE, :], Wb).then_inc(w_loaded, 16)
            sp.dma_start(wbc_nat[STATE:BCR, :], Wc).then_inc(w_loaded, 16)
            sp.dma_start(a_nat, a.rearrange("(h p) r -> p h r", p=P)).then_inc(w_loaded, 16)
            sp.dma_start(b_nat, b_).then_inc(w_loaded, 16)
            for nat, w in ((wg_nat, Wg), (wo_nat, Wo)):
                sp.dma_start(nat, w.rearrange("(h p) d -> p h d", p=P)).then_inc(w_loaded, 16)
            for n4 in range(NQ):
                sp.dma_start(la_nat[Q * n4:Q * n4 + Q],
                             log_a.rearrange("(k p) n -> p k n", p=Q)).then_inc(w_loaded, 16)
            for row, vec in ((brow, bo), (brow2, bias)):
                sp.dma_start(row, vec.rearrange("(o d) -> o d", o=1).broadcast_to([P, D])).then_inc(w_loaded, 16)
            spread(0)
            load_x(2)
            for c in range(NC):
                if c + 3 < NC:
                    load_x(c + 3)
                if c > 0:
                    for j in range(OUTS):
                        load_res(c - 1, j)
                if c + 1 < NC:
                    spread(c + 1)
                if c > 0:
                    for j in range(OUTS):
                        store(c - 1, j)
            for j in range(OUTS):
                load_res(NC - 1, j)
            for j in range(OUTS):
                store(NC - 1, j)
            for s in out_stored:
                sp.wait_ge(s, 16 * NC)

        @block.gpsimd
        def _(pool):
            nc.gpsimd.memset(ident[:], 0.0).then_inc(pool_memsets, 1)
            pool.wait_ge(pool_memsets, 1)
            nc.gpsimd.affine_select(out=ident[:], in_=ident[:], compare_op=ALU.not_equal, fill=1.0, base=0,
                                    pattern=[[-1, P]], channel_multiplier=1).then_inc(ident_made, 1)
            nc.gpsimd.memset(decay[:, :, :, 0:1], 0.0).then_inc(pool_memsets, 1)
            nc.gpsimd.memset(minus_half[:], -0.5).then_inc(pool_memsets, 1)
            pool.wait_ge(pool_memsets, 3)

            def inv_std(c):
                pool.wait_ge(ln_stats, c + 1)
                if c > 0:
                    pool.wait_ge(xn_ready, c)
                nc.gpsimd.tensor_tensor(rstd[:], var_eps[:], minus_half[:], ALU.pow).then_inc(rstd_ready, 1)
                pool.wait_ge(rstd_ready, c + 1)
                nc.gpsimd.tensor_tensor(nmr[:], neg_mean[:], rstd[:], ALU.mult).then_inc(nmr_ready, 1)

            def delta_of(c):
                for h in range(HALVES):
                    pool.wait_ge(sp_ready, HALVES * c + h + 1)
                    nc.gpsimd.tensor_tensor(sp_lin[:, h], sp_lin[:, h], sp_log[:, h],
                                            ALU.add).then_inc(dt_ready, 1)

            def u_of(c):
                for h in range(HALVES):
                    pool.wait_ge(dt_ready, HALVES * c + h + 1)
                    nc.gpsimd.tensor_tensor(sp_log[:, h], sp_lin[:, h], xc[:, c % 2, h],
                                            ALU.mult).then_inc(u_ready, 1)

            def times_c(c, i):
                t = TILES * c + i
                m, h = divmod(i, HALVES)
                if h == 0:
                    bank, n = side_use("C", c, m)
                    pool.wait_ge(side_drained[bank], n + 1)
                if c % ROW_CHUNKS < ROW_CHUNKS - 1:
                    pool.wait_ge(h_ready, TILES * (c // ROW_CHUNKS) + i + 1)
                else:
                    pool.wait_ge(scanned, t + 1)
                steps = hbuf[:, t % RING, :, 1:SEG]
                nc.gpsimd.tensor_tensor(steps, steps, c_sb[:, m].unsqueeze(1).broadcast_to([P, NQ, CH]),
                                        ALU.mult).then_inc(prod_ready, 1)

            inv_std(0)
            pool.wait_ge(absmax_own, 1)
            nc.gpsimd.partition_all_reduce(mx[:, 3:4], mx[:, 2:3], P, RMAX).then_inc(absmax_all, 1)
            inv_std(1)
            for c in range(NC):
                for i in range(TILES):
                    if i == 1 and c + 2 < NC:
                        inv_std(c + 2)
                    if i == 1 and c + 1 < NC:
                        delta_of(c + 1)
                    if i == 2 and c + 1 < NC:
                        u_of(c + 1)
                    times_c(c, i)

        @block.scalar
        def _(act):
            def norm(c):
                act.wait_ge(nmr_ready, c + 1)
                for tt in range(TT):
                    ins = nc.scalar.activation(xin[:, c % 2, tt], xin[:, c % 2, tt], ACT.Identity,
                                               bias=nmr[:, tt:tt + 1], scale=rstd[:, tt:tt + 1])
                ins.then_inc(xn_ready, 1)

            def evict_T(c, h):
                use = front_use("T", c, h)
                wait_filled(act, front_filled, use)
                if h == 0 and c >= XRING:
                    wait_filled(act, side_filled, side_use("E", c - XRING, OUTS - 1))
                nc.scalar.copy(xnT[:, c % XRING, h, PAD:PAD + CH], front[:, use[0]]).then_inc(
                    front_drained[use[0]], 1)

            def pad(c):
                ahead = xnT[:, c % XRING, :, 0:PAD]
                if c % ROW_CHUNKS == 0:
                    nc.scalar.memzero(ahead).then_inc(pad_ready, 1)
                else:
                    nc.scalar.copy(ahead, xnT[:, (c - 1) % XRING, :, CH:CH + PAD]).then_inc(pad_ready, 1)

            def conv_act(c, h):
                use = front_use("V", c, h)
                if c >= 2 and h == 0:
                    act.wait_ge(u_ready, HALVES * (c - 1))
                    wait_filled(act, front_filled, front_use("X", c - 2, 0))
                if c >= 1:
                    act.wait_ge(xc_ready, HALVES * (c - 1) + h + 1)
                wait_filled(act, front_filled, use)
                nc.scalar.activation(xh[:, h], front[:, use[0]], ACT.Identity, bias=cb_col[:, h:h + 1])
                nc.scalar.activation(xc[:, c % 2, h], front[:, use[0]], ACT.Tanh,
                                     bias=cb_col[:, h:h + 1]).then_inc(front_drained[use[0]], 1)

            def softplus(c):
                if c > 0:
                    act.wait_ge(dt_spread, SPREAD * c)
                if c > 1:
                    act.wait_ge(u_spread, SPREAD * (c - 1))
                if c == 1:
                    act.wait_ge(u0_filled, BLOCKS)
                for h in range(HALVES):
                    use = front_use("Z", c, h)
                    wait_filled(act, front_filled, use)
                    nc.scalar.activation(sp_log[:, h], front[:, use[0]], ACT.Abs,
                                         bias=bd_col[:, h:h + 1]).then_inc(sp_abs, 1)
                    nc.scalar.activation(sp_lin[:, h], front[:, use[0]], ACT.Relu,
                                         bias=bd_col[:, h:h + 1]).then_inc(front_drained[use[0]], 1)
                for h in range(HALVES):
                    act.wait_ge(sp_abs, HALVES * c + h + 1)
                    nc.scalar.activation(sp_log[:, h], sp_log[:, h], ACT.Exp, scale=-1.0).then_inc(sp_exp, 1)
                for h in range(HALVES):
                    act.wait_ge(sp_exp, HALVES * c + h + 1)
                    nc.scalar.activation(sp_log[:, h], sp_log[:, h], ACT.Ln, bias=1.0).then_inc(sp_ready, 1)

            def bc_high(c):
                use = front_use("X", c, 0)
                if c >= 2:
                    wait_filled(act, side_filled, side_use("C", c - 2, QUADS - 1))
                wait_filled(act, front_filled, use)
                nc.scalar.copy(bc_parts[:, c % 2], front[0:PARTS * BCR, use[0]]).then_inc(bc_hi, 1)

            def make_decay(c, i):
                t = TILES * c + i
                m, h = divmod(i, HALVES)
                if i == 0:
                    act.wait_ge(dt_spread, SPREAD * (c + 1))
                if t >= 2:
                    act.wait_ge(scanned, t - 1)
                for q in range(NQ):
                    k = NQ * h + q
                    ins = nc.scalar.activation(decay[:, i % 2, q, 1:SEG], dt_rep[:, c % 2, k], ACT.Exp,
                                               scale=a_col[:, k, m:m + 1])
                ins.then_inc(decay_ready, 1)

            def copy_c(c, m):
                use = side_use("C", c, m)
                if c > 0:
                    act.wait_ge(prod_ready, TILES * (c - 1) + HALVES * (m + 1))
                wait_filled(act, side_filled, use)
                nc.scalar.copy(c_sb[:, m], side[:, use[0]]).then_inc(side_drained[use[0]], 1)

            def gate(c, h):
                use = side_use("G", c, h)
                wait_filled(act, side_filled, use)
                nc.scalar.activation(yg[:, h], side[:, use[0]], ACT.Tanh, scale=0.5,
                                     bias=bg_col[:, h:h + 1]).then_inc(side_drained[use[0]], 1)

            pad(0)
            norm(0)
            for h in range(HALVES):
                evict_T(0, h)
            norm(1)
            act.wait_ge(wd_transposed, 1)
            nc.scalar.copy(WdT[:].rearrange("p h d -> p (h d)"), y_ps[:, 0]).then_inc(w_evicted, 1)
            act.wait_ge(cols_halved, 1)
            act.wait_ge(w_loaded, 16 * W_DMAS)
            for n4 in range(NQ):
                src = la_nat[Q * n4:Q * n4 + Q].rearrange("p k (m n) -> p k m n", n=NQ)[:, :, :, n4]
                ins = nc.scalar.activation(a_col[Q * n4:Q * n4 + Q], src, ACT.Exp)
            ins.then_inc(a_exp, 1)
            for h in range(HALVES):
                conv_act(0, h)
            for h in range(HALVES):
                evict_T(1, h)
            pad(1)
            act.wait_ge(w_transposed, 1)
            nc.scalar.copy(WgT[:].rearrange("p h d -> p (h d)"), y_ps[:, 1]).then_inc(w_evicted, 1)
            nc.scalar.mul(WoT[:].rearrange("p h d -> p (h d)"), b_ps[:, 0], 0.5).then_inc(w_evicted, 1)
            softplus(0)
            bc_high(0)
            for h in range(HALVES):
                conv_act(1, h)
            for k in range(0, BLOCKS, 2):
                act.wait_ge(u0_filled, k + 1)
                nc.scalar.copy(u_rep[:, 0, k], y_ps[:, 0]).then_inc(u0_copied[0], 1)
            copy_c(0, 0)
            act.wait_ge(a_ready, 1)
            act.wait_ge(pool_memsets, 2)
            make_decay(0, 0)
            for c in range(NC):
                for i in range(TILES):
                    if i + 1 < TILES:
                        make_decay(c, i + 1)
                    for kind, m in SIDE_SLOTS.get(i, []):
                        if kind == "G" and c > 0:
                            gate(c - 1, m)
                        if kind == "C" and QUADS * c + m < QUADS * NC:
                            copy_c(c + m // QUADS, m % QUADS)
                    if i == 1:
                        if c + 2 < NC:
                            norm(c + 2)
                    if i == 0 and c + 1 < NC:
                        softplus(c + 1)
                    if i == 1 and c + 1 < NC:
                        bc_high(c + 1)
                    if i == 2 and c + 2 < NC:
                        for h in range(HALVES):
                            evict_T(c + 2, h)
                        pad(c + 2)
                    if i == 4 and c + 2 < NC:
                        conv_act(c + 2, 0)
                    if i == 5 and c + 2 < NC:
                        conv_act(c + 2, 1)
                    if i + 1 == TILES and c + 1 < NC:
                        make_decay(c + 1, 0)
            for h in range(HALVES):
                gate(NC - 1, h)

        @block.vector
        def _(dve):
            chain = [0]

            def link(ins):
                chain[0] += 1
                ins.then_inc(dve_chain, 1)
                dve.wait_ge(dve_chain, chain[0])

            def norm_stats(c):
                dve.wait_ge(x_loaded[c % 2], 16 * (c // 2 + 1))
                if c > 0:
                    dve.wait_ge(nmr_ready, c)
                for tt in range(TT):
                    ins = nc.vector.bn_stats(stats[:, tt], xin[:, c % 2, tt])
                ins.then_inc(ln_link, 1)
                dve.wait_ge(ln_link, 2 * c + 1)
                for tt in range(TT):
                    ins = nc.vector.bn_aggr(mv[:, tt], stats[:, tt])
                ins.then_inc(ln_link, 1)
                dve.wait_ge(ln_link, 2 * c + 2)
                nc.vector.tensor_scalar(var_eps[:], mv[:, :, 1], EPS, None, ALU.add)
                nc.vector.tensor_scalar(neg_mean[:], mv[:, :, 0], -1.0, None, ALU.mult).then_inc(ln_stats, 1)

            def silu(c, h):
                bank, n = front_use("V", c, h)
                dve.wait_ge(front_drained[bank], n + 1)
                nc.vector.scalar_tensor_tensor(out=xc[:, c % 2, h], in0=xc[:, c % 2, h], scalar=1.0,
                                               in1=xh[:, h], op0=ALU.add, op1=ALU.mult).then_inc(xc_ready, 1)

            def bc_split(c):
                bank, n = front_use("X", c, 0)
                dve.wait_ge(bc_hi, c + 1)
                nc.vector.tensor_tensor(bc_rest[:], front[0:2 * BCR, bank], bc_parts[0:2 * BCR, c % 2],
                                        ALU.subtract).then_inc(front_drained[bank], 1)
                dve.wait_ge(front_drained[bank], n + 1)
                nc.vector.tensor_copy(bc_parts[0:2 * BCR, c % 2], bc_rest[:]).then_inc(bc_mid, 1)
                dve.wait_ge(bc_mid, c + 1)
                nc.vector.tensor_tensor(bc_parts[0:BCR, c % 2], bc_rest[0:BCR], bc_parts[0:BCR, c % 2],
                                        ALU.subtract).then_inc(bc_ready, 1)

            def times_b(c, i):
                t = TILES * c + i
                m, h = divmod(i, HALVES)
                if i == 0 and c > 0:
                    dve.wait_ge(u_spread, SPREAD * c)
                if i < HALVES and c == 0:
                    for copied in u0_copied:
                        dve.wait_ge(copied, NQ // 2 * (i + 1))
                if h == 0:
                    dve.wait_ge(b_filled, QUADS * c + m + 1)
                if t >= RING:
                    dve.wait_ge(summed, t - RING + 1)
                tile = hbuf[:, t % RING]
                if c % ROW_CHUNKS == 0:
                    nc.vector.memset(tile[:, :, 0:1], 0.0)
                else:
                    nc.vector.tensor_copy(tile[:, :, 0], h_state[:, m, h])
                nc.vector.tensor_tensor(tile[:, :, 1:SEG], u_rep[:, c % 2, NQ * h:NQ * h + NQ],
                                        b_ps[:, m % 2].unsqueeze(1).broadcast_to([P, NQ, CH]),
                                        ALU.mult).then_inc(inp_ready, 1)

            def scan(c, i):
                t = TILES * c + i
                dve.wait_ge(inp_ready, t + 1)
                dve.wait_ge(decay_ready, t + 1)
                tile = hbuf[:, t % RING].rearrange("p s l -> p (s l)")
                nc.vector.tensor_tensor_scan(tile, decay[:, i % 2].rearrange("p s l -> p (s l)"), tile, 0.0,
                                             ALU.mult, ALU.add).then_inc(scanned, 1)

            def keep_state(c, i):
                t = TILES * c + i
                m, h = divmod(i, HALVES)
                dve.wait_ge(scanned, TILES * c + i + 1)
                nc.vector.tensor_copy(h_state[:, m, h], hbuf[:, t % RING, :, CH]).then_inc(h_ready, 1)

            def gate_y(c, h):
                bank, n = side_use("G", c, h)
                dve.wait_ge(side_drained[bank], n + 1)
                dve.wait_ge(summed, TILES * (c + 1) - HALVES + h + 1)
                nc.vector.scalar_tensor_tensor(out=yg[:, h], in0=yg[:, h], scalar=1.0, in1=y_ps[:, h],
                                               op0=ALU.add, op1=ALU.mult).then_inc(y_gated, 1)

            def add_residual(c, j):
                use = side_use("E", c, j)
                wait_filled(dve, side_filled, use)
                dve.wait_ge(xres_loaded[j], 16 * (c + 1))
                io = xres[:, j].rearrange("p t d -> p (t d)")
                nc.vector.tensor_tensor(io, side[:, use[0]], io, ALU.add).then_inc(side_drained[use[0]], 1)

            nc.vector.memset(ones[:], 1.0)
            nc.vector.memset(bias_parts[:], 0.0)
            norm_stats(0)
            dve.wait_ge(cols_loaded, 16 * COLS)
            nc.vector.tensor_scalar(cb_col[:], cb_col[:], 0.5, None, ALU.mult)
            nc.vector.tensor_scalar(bg_col[:], bg_col[:], 0.5, None, ALU.mult).then_inc(cols_halved, 1)
            link(nc.vector.tensor_scalar(cw_col[:], cw_col[:], 0.5, None, ALU.mult))
            dve.wait_ge(ident_made, 1)
            for n in range(HALVES * TAPS):
                h, k = divmod(n, TAPS)
                ins = nc.vector.tensor_scalar(taps[:, n], ident[:], cw_col[:, h, k:k + 1], None, ALU.mult)
            ins.then_inc(taps_made, 1)
            norm_stats(1)
            dve.wait_ge(kern_loaded, 16)
            nc.vector.tensor_reduce(mx[:, 0:1], kern_nat, AX.X, ALU.max)
            link(nc.vector.tensor_reduce(mx[:, 1:2], kern_nat, AX.X, ALU.min))
            nc.vector.scalar_tensor_tensor(out=mx[:, 2:3], in0=mx[:, 1:2], scalar=-1.0, in1=mx[:, 0:1],
                                           op0=ALU.mult, op1=ALU.max).then_inc(absmax_own, 1)
            link(nc.vector.tensor_tensor(pick_f, ident[0:96, 0:32], ident[0:96, 32:64], ALU.add))
            link(nc.vector.tensor_tensor(pick_f, pick_f, ident[0:96, 64:96], ALU.add))
            nc.vector.tensor_copy(pick[:], pick_f.unsqueeze(2).broadcast_to([PARTS * BCR, BCR, Q]))
            nc.vector.tensor_copy(spread_q, ident[:].rearrange("p (q d) -> p q d", q=NQ).unsqueeze(2)
                                  .broadcast_to([P, NQ, NQ, Q]))
            link(nc.vector.tensor_tensor(sum_n4[:], ident[:, 0:Q], ident[:, Q:2 * Q], ALU.add))
            link(nc.vector.tensor_tensor(sum_n4[:], sum_n4[:], ident[:, 2 * Q:3 * Q], ALU.add))
            nc.vector.tensor_tensor(sum_n4[:], sum_n4[:], ident[:, 3 * Q:4 * Q], ALU.add).then_inc(picks_made, 1)
            dve.wait_ge(absmax_all, 1)
            s0, s_neg, s_lo, s_res, s_q, s_inv, ns_hi, ns_lo = (scale[:, i:i + 1] for i in range(8))
            link(nc.vector.tensor_scalar(s0, mx[:, 3:4], 1.0 / QMAX, None, ALU.mult))
            link(nc.vector.tensor_copy(scale_hi[:], s0))
            link(nc.vector.tensor_tensor(s_lo, s0, scale_hi[:], ALU.subtract))
            link(nc.vector.scalar_tensor_tensor(out=s_res, in0=scale_hi[:], scalar=-QMAX, in1=mx[:, 3:4],
                                                op0=ALU.mult, op1=ALU.add))
            link(nc.vector.scalar_tensor_tensor(out=s_res, in0=s_lo, scalar=-QMAX, in1=s_res,
                                                op0=ALU.mult, op1=ALU.add))
            link(nc.vector.scalar_tensor_tensor(out=s_q, in0=s_res, scalar=1.0 / QMAX, in1=s0,
                                                op0=ALU.mult, op1=ALU.add))
            link(nc.vector.reciprocal(s_inv, s_q))
            link(nc.vector.tensor_copy(scale_hi[:], s_q))
            link(nc.vector.tensor_tensor(ns_lo, scale_hi[:], s_q, ALU.subtract))
            link(nc.vector.tensor_scalar(ns_hi, scale_hi[:], -1.0, None, ALU.mult))
            link(nc.vector.tensor_scalar(s_neg, s_q, -1.0, None, ALU.mult))
            link(nc.vector.tensor_scalar(quant, kern_nat, s_inv, None, ALU.mult))
            link(nc.vector.tensor_scalar(q_hi, quant, SPLIT, None, ALU.add))
            link(nc.vector.tensor_scalar(q_hi, q_hi, -SPLIT, None, ALU.add))
            link(nc.vector.tensor_tensor(q_lo, quant, q_hi, ALU.subtract))
            link(nc.vector.scalar_tensor_tensor(out=q_res, in0=q_hi, scalar=ns_hi, in1=kern_nat,
                                                op0=ALU.mult, op1=ALU.add))
            link(nc.vector.scalar_tensor_tensor(out=q_res, in0=q_hi, scalar=ns_lo, in1=q_res,
                                                op0=ALU.mult, op1=ALU.add))
            link(nc.vector.scalar_tensor_tensor(out=q_res, in0=q_lo, scalar=s_neg, in1=q_res,
                                                op0=ALU.mult, op1=ALU.add))
            link(nc.vector.scalar_tensor_tensor(out=quant, in0=q_res, scalar=s_inv, in1=quant,
                                                op0=ALU.mult, op1=ALU.add))
            link(nc.vector.tensor_scalar(quant, quant, ROUND, None, ALU.add))
            link(nc.vector.tensor_scalar(quant, quant, -ROUND, -QMAX - 1.0, ALU.add, ALU.max))
            link(nc.vector.tensor_scalar(quant, quant, QMAX, s_q, ALU.min, ALU.mult))
            for h in range(HALVES):
                silu(0, h)
            dve.wait_ge(bca_transposed, 1)
            for part in range(PARTS):
                ins = nc.vector.tensor_copy(WbcT[:, :, part],
                                            b_ps[:, 1, 0:HALVES * BCR].rearrange("p (h r) -> p h r", h=HALVES))
            ins.then_inc(wbc_evicted, 1)
            nc.vector.tensor_copy(aT, b_ps[0:RANK, 1, 128:128 + D]).then_inc(aT_evicted, 1)
            dve.wait_ge(a_exp, 1)
            nc.vector.tensor_scalar(a_col[:], a_col[:], -1.0, None, ALU.mult).then_inc(a_ready, 1)
            for h in range(HALVES):
                dve.wait_ge(sp_ready, h + 1)
                nc.vector.tensor_tensor(sp_lin[:, h], sp_lin[:, h], sp_log[:, h], ALU.add).then_inc(dt_ready, 1)
            for h in range(HALVES):
                dve.wait_ge(dt_ready, h + 1)
                nc.vector.tensor_tensor(sp_log[:, h], sp_lin[:, h], xc[:, 0, h], ALU.mult).then_inc(u_ready, 1)
            bc_split(0)
            use = side_use("ab", 0, 0)
            wait_filled(dve, side_filled, use)
            nc.vector.tensor_tensor(Wff[:].rearrange("p h d -> p (h d)"), quant, side[:, use[0]],
                                    ALU.add).then_inc(side_drained[use[0]], 1)
            dve.wait_ge(w_loaded, 16 * W_DMAS)
            link(nc.vector.tensor_tensor(brow, brow, brow2, ALU.add))
            link(nc.vector.tensor_copy(b_hi, brow))
            link(nc.vector.tensor_tensor(b_rest, brow, b_hi, ALU.subtract))
            link(nc.vector.tensor_copy(b_mid, b_rest))
            link(nc.vector.tensor_tensor(b_rest2, b_rest, b_mid, ALU.subtract))
            for part, src in enumerate((b_hi, b_mid, b_rest2)):
                r = slice(32 * part, 32 * part + 1)
                ins = nc.vector.tensor_copy(bias_parts[r], src[r].unsqueeze(1).broadcast_to([1, 2, D]))
            ins.then_inc(bias_made, 1)
            for h in range(HALVES):
                silu(1, h)
            for k in range(1, BLOCKS, 2):
                dve.wait_ge(u0_filled, k + 1)
                nc.vector.tensor_copy(u_rep[:, 0, k], y_ps[:, 1]).then_inc(u0_copied[1], 1)

            times_b(0, 0)
            for c in range(NC):
                keeps = c % ROW_CHUNKS < ROW_CHUNKS - 1
                for i in range(TILES):
                    scan(c, i)
                    if i + 1 < TILES:
                        times_b(c, i + 1)
                    if keeps:
                        keep_state(c, i)
                    if c > 0 and i == 2:
                        for h in range(HALVES):
                            gate_y(c - 1, h)
                    if i == 0 and c + 2 < NC:
                        norm_stats(c + 2)
                    if i == 2 and c + 1 < NC:
                        bc_split(c + 1)
                    if i in (5, 6) and c + 2 < NC:
                        silu(c + 2, i - 5)
                    if c > 0 and i == 5:
                        add_residual(c - 1, 0)
                    if c > 0 and i == 7:
                        add_residual(c - 1, 1)
                    if i + 1 == TILES and c + 1 < NC:
                        times_b(c + 1, 0)
            for h in range(HALVES):
                gate_y(NC - 1, h)
            for j in range(OUTS):
                add_residual(NC - 1, j)

        @block.tensor
        def _(pe):
            def transposes(c):
                pe.wait_ge(xn_ready, c + 1)
                for h in range(HALVES):
                    use = front_use("T", c, h)
                    wait_free(pe, front_drained, use)
                    for tt in range(TT):
                        ins = nc.tensor.transpose(front[:, use[0], tt * P:(tt + 1) * P],
                                                  xin[:, c % 2, tt, h * P:(h + 1) * P], ident[:])
                    ins.then_inc(front_filled[use[0]], 1)

            def conv(c, h):
                use = front_use("V", c, h)
                wait_free(pe, front_drained, use)
                pe.wait_ge(pad_ready, c + 1)
                for j in range(TAPS):
                    ins = nc.tensor.matmul(front[:, use[0]], taps[:, h * TAPS + j],
                                           xnT[:, c % XRING, h, j:j + CH], start=(j == 0), stop=(j == TAPS - 1))
                ins.then_inc(front_filled[use[0]], 1)

            def delta(c, e):
                use = front_use("Z", c, e)
                pe.wait_ge(xc_ready, HALVES * (c + 1))
                wait_free(pe, front_drained, use)
                for h in range(HALVES):
                    ins = nc.tensor.matmul(front[:, use[0]], WdT[:, h, e * P:(e + 1) * P], xc[:, c % 2, h],
                                           start=(h == 0), stop=(h == HALVES - 1))
                ins.then_inc(front_filled[use[0]], 1)

            def proj_bc(c):
                use = front_use("X", c, 0)
                wait_free(pe, front_drained, use)
                for h in range(HALVES):
                    ins = nc.tensor.matmul(front[0:PARTS * BCR, use[0]], WbcT[:, h].rearrange("p a r -> p (a r)"),
                                           xc[:, c % 2, h], start=(h == 0), stop=(h == HALVES - 1))
                ins.then_inc(front_filled[use[0]], 1)

            def fill_b(c, m):
                if m == 0:
                    pe.wait_ge(bc_ready, c + 1)
                if QUADS * c + m >= 2:
                    pe.wait_ge(inp_ready, TILES * c + HALVES * (m - 1))
                nc.tensor.matmul(b_ps[:, m % 2], pick[:, NQ * m:NQ * m + NQ].rearrange("r a q -> r (a q)"),
                                 bc_parts[:, c % 2], start=True, stop=True).then_inc(b_filled, 1)

            def fill_c(c, m):
                use = side_use("C", c, m)
                wait_free(pe, side_drained, use)
                row = STATE + NQ * m
                nc.tensor.matmul(side[:, use[0]], pick[:, row:row + NQ].rearrange("r a q -> r (a q)"),
                                 bc_parts[:, c % 2], start=True, stop=True).then_inc(side_filled[use[0]], 1)

            def sum_states(c, i):
                t = TILES * c + i
                m, h = divmod(i, HALVES)
                if m == 0 and c > 0:
                    pe.wait_ge(y_gated, HALVES * (c - 1) + h + 1)
                if c == 0 and m == 0:
                    pe.wait_ge(u0_copied[h], BLOCKS // 2)
                pe.wait_ge(prod_ready, TILES * c + i + 1)
                for q in range(NQ):
                    ins = nc.tensor.matmul(y_ps[Q * q:Q * q + Q, h], sum_n4[:], hbuf[:, t % RING, q, 1:SEG],
                                           start=(m == 0), stop=(m == QUADS - 1))
                ins.then_inc(summed, 1)

            def gate(c, e):
                use = side_use("G", c, e)
                wait_free(pe, side_drained, use)
                for h in range(HALVES):
                    ins = nc.tensor.matmul(side[:, use[0]], WgT[:, h, e * P:(e + 1) * P],
                                           xnT[:, c % XRING, h, PAD:PAD + CH],
                                           start=(h == 0), stop=(h == HALVES - 1))
                ins.then_inc(side_filled[use[0]], 1)

            def out_product(c, j):
                use = side_use("E", c, j)
                wait_free(pe, side_drained, use)
                nc.tensor.matmul(side[:, use[0]], ones[:], bias_parts[:].rearrange("p t d -> p (t d)"),
                                 start=True, stop=False)
                for tt in range(2):
                    tok = (2 * j + tt) * P
                    for h in range(HALVES):
                        nc.tensor.matmul(side[:, use[0], tt * D:(tt + 1) * D],
                                         xnT[:, c % XRING, h, PAD + tok:PAD + tok + P], Wff[:, h],
                                         start=False, stop=False)
                pe.wait_ge(y_gated, HALVES * (c + 1))
                for tt in range(2):
                    tok = (2 * j + tt) * P
                    for h in range(HALVES):
                        ins = nc.tensor.matmul(side[:, use[0], tt * D:(tt + 1) * D], yg[:, h, tok:tok + P],
                                               WoT[:, h], start=False, stop=(tt == 1 and h == HALVES - 1))
                ins.then_inc(side_filled[use[0]], 1)

            def transpose_w(dst, nat):
                for h in range(HALVES):
                    for e in range(HALVES):
                        ins = nc.tensor.transpose(dst[:, h * D + e * P:h * D + (e + 1) * P],
                                                  nat[:, e, h * P:(h + 1) * P], ident[:])
                return ins

            pe.wait_ge(ident_made, 1)
            transposes(0)
            pe.wait_ge(wd_loaded, 16)
            transpose_w(y_ps[:, 0], wd_nat).then_inc(wd_transposed, 1)
            pe.wait_ge(taps_made, 1)
            for h in range(HALVES):
                conv(0, h)
            transposes(1)
            pe.wait_ge(w_loaded, 16 * W_DMAS)
            for h in range(HALVES):
                nc.tensor.transpose(b_ps[:, 1, h * BCR:(h + 1) * BCR], wbc_nat[:, h * P:(h + 1) * P],
                                    ident[0:BCR, 0:BCR])
            for h in range(HALVES):
                ins = nc.tensor.transpose(b_ps[0:RANK, 1, 128 + h * P:128 + (h + 1) * P], a_nat[:, h], ident[:])
            ins.then_inc(bca_transposed, 1)
            transpose_w(y_ps[:, 1], wg_nat)
            transpose_w(b_ps[:, 0], wo_nat).then_inc(w_transposed, 1)
            pe.wait_ge(w_evicted, 1)
            for e in range(HALVES):
                delta(0, e)
            pe.wait_ge(wbc_evicted, 1)
            proj_bc(0)
            pe.wait_ge(aT_evicted, 1)
            use = side_use("ab", 0, 0)
            for h in range(HALVES):
                ins = nc.tensor.matmul(side[:, use[0], h * D:(h + 1) * D], aT[:, h * P:(h + 1) * P], b_nat,
                                       start=True, stop=True)
            ins.then_inc(side_filled[use[0]], 1)
            for h in range(HALVES):
                conv(1, h)
            pe.wait_ge(w_evicted, 3)
            for k in range(BLOCKS):
                h, q = divmod(k, NQ)
                pe.wait_ge(u_ready, h + 1)
                if k == 0:
                    pe.wait_ge(picks_made, 1)
                if k >= 2:
                    pe.wait_ge(u0_copied[k % 2], k // 2)
                nc.tensor.matmul(y_ps[:, k % 2], spread_q[:, q].rearrange("p n d -> p (n d)"),
                                 sp_log[:, h], start=True, stop=True).then_inc(u0_filled, 1)
            fill_b(0, 0)
            fill_c(0, 0)

            for c in range(NC):
                for i in range(TILES):
                    t = TILES * c + i
                    if i % HALVES == 0 and t + 2 < TILES * NC:
                        m = i // HALVES + 1
                        fill_b(c + m // QUADS, m % QUADS)
                    for kind, m in SIDE_SLOTS.get(i, []):
                        if kind == "C" and QUADS * c + m < QUADS * NC:
                            fill_c(c + m // QUADS, m % QUADS)
                        if kind == "G" and c > 0:
                            gate(c - 1, m)
                    if t >= 3:
                        sum_states((t - 3) // TILES, (t - 3) % TILES)
                    for kind, k in FRONT_SLOTS.get(i, []):
                        if kind == "Z" and c + 1 < NC:
                            delta(c + 1, k)
                        if kind == "T" and k == 0 and c + 2 < NC:
                            transposes(c + 2)
                        if kind == "X" and c + 1 < NC:
                            proj_bc(c + 1)
                        if kind == "V" and c + 2 < NC:
                            conv(c + 2, k)
                    for kind, j in SIDE_SLOTS.get(i, []):
                        if kind == "E" and c > 0:
                            if c == 1 and j == 0:
                                pe.wait_ge(bias_made, 1)
                            out_product(c - 1, j)
            for e in range(HALVES):
                gate(NC - 1, e)
            for i in range(TILES - 3, TILES):
                sum_states(NC - 1, i)
            for j in range(OUTS):
                out_product(NC - 1, j)


_INS = ['L0_attn_x', 'L0_attn_conv_w', 'L0_attn_conv_b', 'L0_attn_Wd', 'L0_attn_bd', 'L0_attn_Wb', 'L0_attn_Wc',
        'L0_attn_log_a', 'L0_attn_Wg', 'L0_attn_bg', 'L0_attn_Wo', 'L0_attn_bo', 'L0_ffn_kernel', 'L0_ffn_bias',
        'L0_ffn_a', 'L0_ffn_b']


def kernel(**inputs):
    import numpy as _np
    import concourse.bacc as _bacc
    from concourse import mybir as _mybir
    from concourse.bass_utils import run_bass_kernel_spmd as _run

    nc = _bacc.Bacc("TRN2", target_bir_lowering=False, num_devices=1)
    arrays, args = {}, []
    for name in _INS:
        v = _np.ascontiguousarray(inputs[name])
        arrays[f"in_{name}_dram"] = v
        args.append(nc.dram_tensor(f"in_{name}_dram", v.shape, _mybir.dt.from_np(v.dtype), kind="ExternalInput").ap())
    shape = inputs['L0_attn_x'].shape
    args.append(nc.dram_tensor("out_0_dram", shape, _mybir.dt.float32, kind="ExternalOutput").ap())
    build_layer(nc, *args)
    r = _run(nc, [arrays], core_ids=[0])
    return r.results[0]["out_0_dram"]
```

```python
from contextlib import ExitStack

import concourse.bass as bass
from concourse import mybir

ALU = mybir.AluOpType
ACT = mybir.ActivationFunctionType
AX = mybir.AxisListType
F32 = mybir.dt.float32
BF16 = mybir.dt.bfloat16
RMAX = bass.bass_isa.ReduceOp.max

P = 128
Q = 32
ROUND = 12582912.0
SPLIT = 6144.0
QMAX = 7.0
EPS = 1e-5
TILES = 8

FRONT_SLOTS = {0: [("T", 0), ("T", 1)], 1: [("V", 0)], 2: [("V", 1)], 3: [("X", 0)], 5: [("Z", 0), ("Z", 1)]}
AHEAD = {"T": 2, "V": 2, "Z": 2, "X": 1}
SIDE_SLOTS = {0: [("G", -1, 0)], 1: [("C", 0, 1), ("G", -1, 1)], 3: [("C", 0, 2)], 4: [("E", -1, 0)],
              5: [("C", 0, 3)], 7: [("C", 1, 0), ("E", -1, 1)]}
LAST_SIDE_SLOTS = {0: [("G", -1, 0)], 1: [("C", 0, 1), ("G", -1, 1)], 2: [("C", 0, 2)],
                   3: [("C", 0, 3), ("E", -1, 0)], 4: [("E", -1, 1)], 5: [("G", 0, 0)],
                   6: [("G", 0, 1), ("E", 0, 0)]}
OUT_SLOTS = {0: [(-2, 1)], 5: [(-1, 0)]}
LAST_OUT_SLOTS = {0: [(-2, 1)], 4: [(-1, 0)], 5: [(-1, 1)]}


def build_layer(nc, x, conv_w, conv_b, Wd, bd, Wb, Wc, log_a, Wg, bg, Wo, bo, kern, bias, a, b_, out):
    NB, L, D = x.shape
    STATE = Wb.shape[0]
    TAPS = conv_w.shape[2]
    RANK = a.shape[1]
    PAD = TAPS - 1
    HALVES = D // P
    NQ = P // Q
    BLOCKS = HALVES * NQ
    QUADS = STATE // NQ
    CH = 512
    ROW_CHUNKS = L // CH
    NC = NB * ROW_CHUNKS
    TT = CH // P
    SEG = CH + 1
    RING = 5
    XRING = 4
    PARTS = 3
    BCR = 2 * STATE
    OUTS = TT // 2
    assert HALVES == 2 and QUADS * HALVES == TILES and BCR == 32 and ROW_CHUNKS == 2

    front_uses = [("T", 0, h) for h in range(HALVES)] + [("V", 0, h) for h in range(HALVES)]
    front_uses += [("T", 1, 0), ("T", 1, 1), ("Z", 0, 0), ("Z", 0, 1), ("X", 0, 0), ("V", 1, 0), ("V", 1, 1)]

    def side_slot(c, slot):
        table = SIDE_SLOTS if c < NC - 1 else LAST_SIDE_SLOTS
        return [(kind, c + at, i) for kind, at, i in table.get(slot, []) if 0 <= c + at < NC]

    def out_slot(c, slot):
        table = OUT_SLOTS if c < NC - 1 else LAST_OUT_SLOTS
        return [(c + at, j) for at, j in table.get(slot, []) if c + at >= 0]

    side_uses = [("ab", 0, 0), ("C", 0, 0)]
    for c in range(NC):
        for slot in range(TILES):
            front_uses += [(kind, c + AHEAD[kind], i) for kind, i in FRONT_SLOTS.get(slot, [])
                           if c + AHEAD[kind] < NC]
            if c == 0 and slot == 0:
                front_uses += [("Z", 1, 0), ("Z", 1, 1)]
            side_uses += side_slot(c, slot)
    side_uses.append(("E", NC - 1, 1))

    def front_use(kind, c, i):
        return divmod(front_uses.index((kind, c, i)), 2)[::-1]

    def side_use(kind, c, i):
        return divmod(side_uses.index((kind, c, i)), 2)[::-1]

    with ExitStack() as ctx:
        def sb(name, shape, dt=F32):
            return ctx.enter_context(nc.sbuf_tensor(name, shape, dt))

        def pb(name, shape, dt=F32):
            return ctx.enter_context(nc.psum_tensor(name, shape, dt))

        def sem(name):
            return ctx.enter_context(nc.semaphore(name))

        dt_rep = sb("dt_rep", [P, 2, BLOCKS, CH])
        u_rep = sb("u_rep", [P, 2, BLOCKS, CH])
        bc_parts = sb("bc_parts", [PARTS * BCR, 2, CH], BF16)
        c_sb = sb("c_sb", [P, QUADS, CH])
        xnT = sb("xnT", [P, XRING, HALVES, PAD + CH])
        decay = sb("decay", [P, 2, NQ, SEG])
        hbuf = sb("hbuf", [P, RING, NQ, SEG])
        h_state = sb("h_state", [P, QUADS, HALVES, NQ])
        yg = sb("yg", [P, HALVES, CH])
        xin = sb("xin", [P, 2, TT, D])
        xh = sb("xh", [P, HALVES, CH])
        xc = sb("xc", [P, 2, HALVES, CH])
        sp_log = sb("sp_log", [P, HALVES, CH])
        sp_lin = sb("sp_lin", [P, HALVES, CH])
        bc_rest = sb("bc_rest", [2 * BCR, CH])
        xres = sb("xres", [P, OUTS, 2, D])
        WdT = sb("WdT", [P, HALVES, D])
        WgT = sb("WgT", [P, HALVES, D])
        WoT = sb("WoT", [P, HALVES, D])
        Wff = sb("Wff", [P, HALVES, D])
        WbcT = sb("WbcT", [P, HALVES, PARTS, BCR])
        taps = sb("taps", [P, HALVES * TAPS, P])
        ident = sb("ident", [P, P])
        sum_n4 = sb("sum_n4", [P, Q])
        pick = sb("pick", [PARTS * BCR, BCR, Q], BF16)
        bias_parts = sb("bias_parts", [P, 2, D], BF16)
        ones = sb("ones", [P, P], BF16)
        a_col = sb("a_col", [P, BLOCKS, QUADS])
        bd_col = sb("bd_col", [P, HALVES])
        bg_col = sb("bg_col", [P, HALVES])
        cb_col = sb("cb_col", [P, HALVES])
        cw_col = sb("cw_col", [P, HALVES, TAPS])
        stats = sb("stats", [P, TT, 6])
        mv = sb("mv", [P, TT, 2])
        var_eps = sb("var_eps", [P, TT])
        neg_mean = sb("neg_mean", [P, TT])
        minus_half = sb("minus_half", [P, TT])
        rstd = sb("rstd", [P, TT])
        nmr = sb("nmr", [P, TT])
        mx = sb("mx", [P, 4])
        scale_hi = sb("scale_hi", [P, 1], BF16)
        scale = sb("scale", [P, 8])

        room = u_rep[:, 1].rearrange("p b t -> p (b t)")
        wd_nat = room[:, 0:512].rearrange("p (h d) -> p h d", h=2)
        wg_nat = room[:, 512:1024].rearrange("p (h d) -> p h d", h=2)
        wo_nat = room[:, 1024:1536].rearrange("p (h d) -> p h d", h=2)
        kern_nat = room[:, 1536:2048]
        quant = room[:, 2048:2560]
        q_hi = room[:, 2560:3072]
        q_lo = room[:, 3072:3584]
        q_res = room[:, 3584:4096]
        room2 = dt_rep[:, 1].rearrange("p b t -> p (b t)")
        wbc_nat = room2[0:BCR, 0:D]
        a_nat = room2[:, 256:256 + HALVES * RANK].rearrange("p (h r) -> p h r", h=HALVES)
        b_nat = room2[0:RANK, 512:512 + D]
        aT = room2[0:RANK, 768:768 + D]
        la_nat = room2[:, 1024:1024 + BLOCKS * STATE].rearrange("p (k n) -> p k n", k=BLOCKS)
        pick_f = room2[0:PARTS * BCR, 1152:1152 + BCR]
        brow = room2[:, 1280:1536]
        brow2 = room2[:, 1536:1792]
        b_hi = room2[:, 1792:1920].bitcast(BF16)
        b_mid = room2[:, 1920:2048].bitcast(BF16)
        b_rest = room2[:, 2048:2304]
        b_rest2 = room2[:, 2304:2560]
        spread_q = room2[:, 2560:2560 + NQ * P].rearrange("p (q n d) -> p q n d", q=NQ, n=NQ)

        y_ps = pb("y_ps", [P, HALVES, CH])
        b_ps = pb("b_ps", [P, 2, CH])
        side = pb("side", [P, 2, CH])
        front = pb("front", [P, 2, CH])

        dt0_banks = (b_ps[:, 1], side[:, 0])

        cols_loaded = sem("cols_loaded")
        kern_loaded = sem("kern_loaded")
        wd_loaded = sem("wd_loaded")
        w_loaded = sem("w_loaded")
        ident_made = sem("ident_made")
        pool_memsets = sem("pool_memsets")
        dve_chain = sem("dve_chain")
        absmax_all = sem("absmax_all")
        absmax_own = sem("absmax_own")
        wd_transposed = sem("wd_transposed")
        bca_transposed = sem("bca_transposed")
        w_transposed = sem("w_transposed")
        w_evicted = sem("w_evicted")
        wbc_evicted = sem("wbc_evicted")
        aT_evicted = sem("aT_evicted")
        a_exp = sem("a_exp")
        a_ready = sem("a_ready")
        cols_halved = sem("cols_halved")
        taps_made = sem("taps_made")
        picks_made = sem("picks_made")
        bias_made = sem("bias_made")
        u0_filled = sem("u0_filled")
        dt0_filled = sem("dt0_filled")
        dt0_used = sem("dt0_used")
        u0_copied = [sem(f"u0_copied{i}") for i in range(2)]
        x_loaded = [sem(f"x_loaded{i}") for i in range(2)]
        ln_stats = sem("ln_stats")
        ln_link = sem("ln_link")
        rstd_ready = sem("rstd_ready")
        nmr_ready = sem("nmr_ready")
        xn_ready = sem("xn_ready")
        pad_ready = sem("pad_ready")
        front_filled = [sem(f"front_filled{i}") for i in range(2)]
        front_drained = [sem(f"front_drained{i}") for i in range(2)]
        xc_ready = sem("xc_ready")
        sp_abs = sem("sp_abs")
        sp_exp = sem("sp_exp")
        sp_ready = sem("sp_ready")
        dt_ready = sem("dt_ready")
        u_ready = sem("u_ready")
        bc_hi = sem("bc_hi")
        bc_mid = sem("bc_mid")
        bc_ready = sem("bc_ready")
        dt_spread = sem("dt_spread")
        u_spread = sem("u_spread")
        b_filled = sem("b_filled")
        side_filled = [sem(f"side_filled{i}") for i in range(2)]
        side_drained = [sem(f"side_drained{i}") for i in range(2)]
        decay_ready = sem("decay_ready")
        inp_ready = sem("inp_ready")
        scanned = sem("scanned")
        h_ready = sem("h_ready")
        prod_ready = sem("prod_ready")
        last_prod_ready = sem("last_prod_ready")
        summed = sem("summed")
        y_gated = sem("y_gated")
        xres_loaded = [sem(f"xres_loaded{i}") for i in range(OUTS)]
        out_stored = [sem(f"out_stored{i}") for i in range(OUTS)]
        SPREAD = 16 * NQ * NQ
        COLS = 4
        W_DMAS = 12

        x_chunk = x.rearrange("b (c t p) d -> (b c) p t d", p=P, c=ROW_CHUNKS)
        x_pair = x.rearrange("b (j t p) d -> (b j) p t d", p=P, t=2)
        out_pair = out.rearrange("b (j t p) d -> (b j) p t d", p=P, t=2)

        def wait_filled(eng, sems, use):
            bank, n = use
            eng.wait_ge(sems[bank], n + 1)

        def wait_free(eng, sems, use):
            bank, n = use
            if n > 0:
                eng.wait_ge(sems[bank], n)

        block = ctx.enter_context(nc.Block())

        @block.sync
        def _(sp):
            def load_x(c):
                if c >= 2:
                    wait_filled(sp, front_filled, front_use("T", c - 2, 1))
                sp.dma_start(xin[:, c % 2], x_chunk[c]).then_inc(x_loaded[c % 2], 16)

            def to_states(made, rep, c, done):
                for q in range(NQ):
                    for n4 in range(NQ):
                        dst = rep[Q * n4:Q * n4 + Q, c % 2, q:q + NQ + 1:NQ]
                        sp.dma_start(dst, made[Q * q:Q * q + Q]).then_inc(done, 16)

            def spread_dt(c):
                sp.wait_ge(dt_ready, HALVES * (c + 1))
                if c > 1:
                    sp.wait_ge(decay_ready, TILES * (c - 1))
                to_states(sp_lin, dt_rep, c, dt_spread)

            def spread_u(c):
                sp.wait_ge(u_ready, HALVES * (c + 1))
                if c > 1:
                    sp.wait_ge(inp_ready, TILES * (c - 1))
                to_states(sp_log, u_rep, c, u_spread)

            def load_res(c, j):
                if c > 0:
                    sp.wait_ge(out_stored[j], 16 * c)
                sp.dma_start(xres[:, j], x_pair[OUTS * c + j]).then_inc(xres_loaded[j], 16)

            def store(c, j):
                bank, n = side_use("E", c, j)
                sp.wait_ge(side_drained[bank], n + 1)
                sp.dma_start(out_pair[OUTS * c + j], xres[:, j]).then_inc(out_stored[j], 16)

            load_x(0)
            sp.dma_start(cw_col[:], conv_w.rearrange("(h p) o k -> p h (o k)", p=P)).then_inc(cols_loaded, 16)
            for col, vec in ((cb_col, conv_b), (bd_col, bd), (bg_col, bg)):
                sp.dma_start(col[:], vec.rearrange("(h p) -> p h", p=P),
                             allow_slow_non_contiguous=True).then_inc(cols_loaded, 16)
            sp.dma_start(kern_nat.rearrange("p (h f) -> p h f", h=HALVES),
                         kern.rearrange("(h p) f -> p h f", p=P)).then_inc(kern_loaded, 16)
            load_x(1)
            sp.dma_start(wd_nat, Wd.rearrange("(h p) d -> p h d", p=P)).then_inc(wd_loaded, 16)
            sp.dma_start(wbc_nat[0:STATE, :], Wb).then_inc(w_loaded, 16)
            sp.dma_start(wbc_nat[STATE:BCR, :], Wc).then_inc(w_loaded, 16)
            sp.dma_start(a_nat, a.rearrange("(h p) r -> p h r", p=P)).then_inc(w_loaded, 16)
            sp.dma_start(b_nat, b_).then_inc(w_loaded, 16)
            for nat, w in ((wg_nat, Wg), (wo_nat, Wo)):
                sp.dma_start(nat, w.rearrange("(h p) d -> p h d", p=P)).then_inc(w_loaded, 16)
            for n4 in range(NQ):
                sp.dma_start(la_nat[Q * n4:Q * n4 + Q],
                             log_a.rearrange("(k p) n -> p k n", p=Q)).then_inc(w_loaded, 16)
            for row, vec in ((brow, bo), (brow2, bias)):
                sp.dma_start(row, vec.rearrange("(o d) -> o d", o=1).broadcast_to([P, D])).then_inc(w_loaded, 16)
            load_x(2)
            load_x(3)
            spread_dt(0)
            for c in range(NC):
                if c > 0:
                    load_res(c - 1, 0)
                if c + 1 < NC:
                    spread_dt(c + 1)
                if c > 1:
                    store(c - 2, 1)
                if c > 0:
                    load_res(c - 1, 1)
                if c + 1 < NC:
                    spread_u(c + 1)
                if c + 4 < NC:
                    load_x(c + 4)
                if c > 0:
                    store(c - 1, 0)
            load_res(NC - 1, 0)
            store(NC - 2, 1)
            load_res(NC - 1, 1)
            for j in range(OUTS):
                store(NC - 1, j)
            for s in out_stored:
                sp.wait_ge(s, 16 * NC)

        @block.gpsimd
        def _(pool):
            nc.gpsimd.memset(ident[:], 0.0).then_inc(pool_memsets, 1)
            pool.wait_ge(pool_memsets, 1)
            nc.gpsimd.affine_select(out=ident[:], in_=ident[:], compare_op=ALU.not_equal, fill=1.0, base=0,
                                    pattern=[[-1, P]], channel_multiplier=1).then_inc(ident_made, 1)
            nc.gpsimd.memset(decay[:, :, :, 0:1], 0.0).then_inc(pool_memsets, 1)
            nc.gpsimd.memset(minus_half[:], -0.5).then_inc(pool_memsets, 1)
            pool.wait_ge(pool_memsets, 3)

            def inv_std(c):
                pool.wait_ge(ln_stats, c + 1)
                if c > 0:
                    pool.wait_ge(xn_ready, c)
                nc.gpsimd.tensor_tensor(rstd[:], var_eps[:], minus_half[:], ALU.pow).then_inc(rstd_ready, 1)
                pool.wait_ge(rstd_ready, c + 1)
                nc.gpsimd.tensor_tensor(nmr[:], neg_mean[:], rstd[:], ALU.mult).then_inc(nmr_ready, 1)

            def delta_of(c):
                for h in range(HALVES):
                    pool.wait_ge(sp_ready, HALVES * c + h + 1)
                    nc.gpsimd.tensor_tensor(sp_lin[:, h], sp_lin[:, h], sp_log[:, h],
                                            ALU.add).then_inc(dt_ready, 1)

            def u_of(c):
                for h in range(HALVES):
                    pool.wait_ge(dt_ready, HALVES * c + h + 1)
                    nc.gpsimd.tensor_tensor(sp_log[:, h], sp_lin[:, h], xc[:, c % 2, h],
                                            ALU.mult).then_inc(u_ready, 1)

            def times_c(c, i):
                t = TILES * c + i
                m, h = divmod(i, HALVES)
                if h == 0:
                    bank, n = side_use("C", c, m)
                    pool.wait_ge(side_drained[bank], n + 1)
                if c % ROW_CHUNKS < ROW_CHUNKS - 1:
                    pool.wait_ge(h_ready, TILES * (c // ROW_CHUNKS) + i + 1)
                else:
                    pool.wait_ge(scanned, t + 1)
                steps = hbuf[:, t % RING, :, 1:SEG]
                nc.gpsimd.tensor_tensor(steps, steps, c_sb[:, m].unsqueeze(1).broadcast_to([P, NQ, CH]),
                                        ALU.mult).then_inc(prod_ready, 1)

            inv_std(0)
            pool.wait_ge(absmax_own, 1)
            nc.gpsimd.partition_all_reduce(mx[:, 3:4], mx[:, 2:3], P, RMAX).then_inc(absmax_all, 1)
            inv_std(1)
            inv_std(2)
            for c in range(NC):
                for i in range(TILES):
                    if i == 2 and c + 3 < NC:
                        inv_std(c + 3)
                    if c == 0 and i == 2:
                        delta_of(1)
                        u_of(1)
                    if c == 1 and i == 1:
                        delta_of(2)
                        u_of(2)
                    if i == 7 and 0 < c < NC - 2:
                        delta_of(c + 2)
                    if i == 0 and 1 < c < NC - 1:
                        u_of(c + 1)
                    if TILES * c + i + 1 < TILES * NC:
                        times_c(c, i)

        @block.scalar
        def _(act):
            def norm(c):
                act.wait_ge(nmr_ready, c + 1)
                for tt in range(TT):
                    ins = nc.scalar.activation(xin[:, c % 2, tt], xin[:, c % 2, tt], ACT.Identity,
                                               bias=nmr[:, tt:tt + 1], scale=rstd[:, tt:tt + 1])
                ins.then_inc(xn_ready, 1)

            def evict_T(c, h):
                use = front_use("T", c, h)
                wait_filled(act, front_filled, use)
                if h == 0 and c >= XRING:
                    wait_filled(act, side_filled, side_use("E", c - XRING, OUTS - 1))
                nc.scalar.copy(xnT[:, c % XRING, h, PAD:PAD + CH], front[:, use[0]]).then_inc(
                    front_drained[use[0]], 1)

            def pad(c):
                ahead = xnT[:, c % XRING, :, 0:PAD]
                if c % ROW_CHUNKS == 0:
                    nc.scalar.memzero(ahead).then_inc(pad_ready, 1)
                else:
                    nc.scalar.copy(ahead, xnT[:, (c - 1) % XRING, :, CH:CH + PAD]).then_inc(pad_ready, 1)

            def conv_act(c, h):
                use = front_use("V", c, h)
                if c >= 2 and h == 0:
                    act.wait_ge(u_ready, HALVES * (c - 1))
                    wait_filled(act, front_filled, front_use("X", c - 2, 0))
                if c >= 1:
                    act.wait_ge(xc_ready, HALVES * (c - 1) + h + 1)
                wait_filled(act, front_filled, use)
                nc.scalar.activation(xh[:, h], front[:, use[0]], ACT.Identity, bias=cb_col[:, h:h + 1])
                nc.scalar.activation(xc[:, c % 2, h], front[:, use[0]], ACT.Tanh,
                                     bias=cb_col[:, h:h + 1]).then_inc(front_drained[use[0]], 1)

            def softplus_exp(c, h):
                if c > 0 and h == 0:
                    act.wait_ge(dt_spread, SPREAD * c)
                if c > 1 and h == 0:
                    act.wait_ge(u_spread, SPREAD * (c - 1))
                if c == 1 and h == 0:
                    act.wait_ge(u0_filled, BLOCKS)
                use = front_use("Z", c, h)
                wait_filled(act, front_filled, use)
                nc.scalar.activation(sp_log[:, h], front[:, use[0]], ACT.Abs,
                                     bias=bd_col[:, h:h + 1]).then_inc(sp_abs, 1)
                nc.scalar.activation(sp_lin[:, h], front[:, use[0]], ACT.Relu,
                                     bias=bd_col[:, h:h + 1]).then_inc(front_drained[use[0]], 1)
                act.wait_ge(sp_abs, HALVES * c + h + 1)
                nc.scalar.activation(sp_log[:, h], sp_log[:, h], ACT.Exp, scale=-1.0).then_inc(sp_exp, 1)

            def softplus_log(c):
                for h in range(HALVES):
                    act.wait_ge(sp_exp, HALVES * c + h + 1)
                    nc.scalar.activation(sp_log[:, h], sp_log[:, h], ACT.Ln, bias=1.0).then_inc(sp_ready, 1)

            def bc_high(c):
                use = front_use("X", c, 0)
                if c >= 2:
                    wait_filled(act, side_filled, side_use("C", c - 2, QUADS - 1))
                wait_filled(act, front_filled, use)
                nc.scalar.copy(bc_parts[:, c % 2], front[0:PARTS * BCR, use[0]]).then_inc(bc_hi, 1)

            def bc_middle(c):
                bank, n = front_use("X", c, 0)
                act.wait_ge(front_drained[bank], n + 1)
                nc.scalar.copy(bc_parts[0:2 * BCR, c % 2], bc_rest[:]).then_inc(bc_mid, 1)

            def make_decay(c, i):
                t = TILES * c + i
                m, h = divmod(i, HALVES)
                if i == (0 if c > 0 else 1):
                    act.wait_ge(dt_spread, SPREAD * (c + 1))
                if t >= 2:
                    act.wait_ge(scanned, t - 1)
                for q in range(NQ):
                    k = NQ * h + q
                    ins = nc.scalar.activation(decay[:, i % 2, q, 1:SEG], dt_rep[:, c % 2, k], ACT.Exp,
                                               scale=a_col[:, k, m:m + 1])
                ins.then_inc(decay_ready, 1)

            def copy_c(c, m):
                use = side_use("C", c, m)
                if c > 0:
                    act.wait_ge(prod_ready, TILES * (c - 1) + HALVES * (m + 1))
                wait_filled(act, side_filled, use)
                nc.scalar.copy(c_sb[:, m], side[:, use[0]]).then_inc(side_drained[use[0]], 1)

            def gate(c, h):
                use = side_use("G", c, h)
                wait_filled(act, side_filled, use)
                nc.scalar.activation(yg[:, h], side[:, use[0]], ACT.Tanh, scale=0.5,
                                     bias=bg_col[:, h:h + 1]).then_inc(side_drained[use[0]], 1)

            def drain_out(c, j):
                use = side_use("E", c, j)
                wait_filled(act, side_filled, use)
                nc.scalar.copy(xres[:, j].rearrange("p t d -> p (t d)"), side[:, use[0]]).then_inc(
                    side_drained[use[0]], 1)

            pad(0)
            norm(0)
            for h in range(HALVES):
                evict_T(0, h)
            norm(1)
            act.wait_ge(wd_transposed, 1)
            nc.scalar.copy(WdT[:].rearrange("p h d -> p (h d)"), y_ps[:, 0]).then_inc(w_evicted, 1)
            act.wait_ge(cols_halved, 1)
            for h in range(HALVES):
                conv_act(0, h)
            for h in range(HALVES):
                evict_T(1, h)
            pad(1)
            act.wait_ge(w_transposed, 1)
            nc.scalar.copy(WgT[:].rearrange("p h d -> p (h d)"), y_ps[:, 1]).then_inc(w_evicted, 1)
            nc.scalar.mul(WoT[:].rearrange("p h d -> p (h d)"), b_ps[:, 0], 0.5).then_inc(w_evicted, 1)
            for h in range(HALVES):
                softplus_exp(0, h)
            bc_high(0)
            softplus_log(0)
            bc_middle(0)
            act.wait_ge(w_loaded, 16 * W_DMAS)
            for n4 in range(NQ):
                src = la_nat[Q * n4:Q * n4 + Q].rearrange("p k (m n) -> p k m n", n=NQ)[:, :, :, n4]
                ins = nc.scalar.activation(a_col[Q * n4:Q * n4 + Q], src, ACT.Exp)
            ins.then_inc(a_exp, 1)

            def copy_u0(k):
                act.wait_ge(u0_filled, k + 1)
                nc.scalar.copy(u_rep[:, 0, k], y_ps[:, 0]).then_inc(u0_copied[0], 1)

            copy_u0(0)
            norm(2)
            copy_u0(2)
            act.wait_ge(a_ready, 1)
            act.wait_ge(pool_memsets, 2)
            for q in range(NQ):
                act.wait_ge(dt0_filled, q + 1)
                nc.scalar.activation(decay[:, 0, q, 1:SEG], dt0_banks[q % 2], ACT.Exp, scale=a_col[:, q, 0:1]
                                     ).then_inc(dt0_used if q < NQ - 1 else decay_ready, 1)
            copy_u0(4)
            copy_u0(6)
            copy_c(0, 0)
            conv_act(1, 0)
            for c in range(NC):
                for i in range(TILES):
                    if i + 1 < TILES:
                        make_decay(c, i + 1)
                    if i == 5 and c + 1 < NC:
                        bc_middle(c + 1)
                    for chunk, j in out_slot(c, i):
                        drain_out(chunk, j)
                    if i == 1 and c == 0:
                        for h in range(HALVES):
                            softplus_exp(1, h)
                    if i in (2, 3) and c + 2 < NC:
                        conv_act(c + 2, i - 2)
                    for kind, chunk, m in side_slot(c, i):
                        if kind == "G":
                            gate(chunk, m)
                        if kind == "C":
                            copy_c(chunk, m)
                    if i == 0 and c == 0:
                        conv_act(1, 1)
                    if i == 2 and c == 0:
                        softplus_log(1)
                    if i == 0 and c == 1:
                        softplus_log(2)
                    if i == 0 and c + 2 < NC:
                        for h in range(HALVES):
                            evict_T(c + 2, h)
                        pad(c + 2)
                    if i == 3 and c + 1 < NC:
                        bc_high(c + 1)
                    if i == 4 and c + 3 < NC:
                        norm(c + 3)
                    late = 1 if c == 1 else 0
                    if i in (5 + late, 6 + late) and 0 < c < NC - 2:
                        softplus_exp(c + 2, i - 5 - late)
                    if i == 7 and 0 < c < NC - 2:
                        softplus_log(c + 2)
                    if i + 1 == TILES and c + 1 < NC:
                        make_decay(c + 1, 0)
                    if i == 7 and c == 0:
                        for h in range(HALVES):
                            softplus_exp(2, h)
            for j in range(OUTS):
                drain_out(NC - 1, j)

        @block.vector
        def _(dve):
            chain = [0]

            def link(ins):
                chain[0] += 1
                ins.then_inc(dve_chain, 1)
                dve.wait_ge(dve_chain, chain[0])

            def norm_stats(c):
                dve.wait_ge(x_loaded[c % 2], 16 * (c // 2 + 1))
                if c > 0:
                    dve.wait_ge(nmr_ready, c)
                for tt in range(TT):
                    ins = nc.vector.bn_stats(stats[:, tt], xin[:, c % 2, tt])
                ins.then_inc(ln_link, 1)
                dve.wait_ge(ln_link, 2 * c + 1)
                for tt in range(TT):
                    ins = nc.vector.bn_aggr(mv[:, tt], stats[:, tt])
                ins.then_inc(ln_link, 1)
                dve.wait_ge(ln_link, 2 * c + 2)
                nc.vector.tensor_scalar(var_eps[:], mv[:, :, 1], EPS, None, ALU.add)
                nc.vector.tensor_scalar(neg_mean[:], mv[:, :, 0], -1.0, None, ALU.mult).then_inc(ln_stats, 1)

            def silu(c, h):
                bank, n = front_use("V", c, h)
                dve.wait_ge(front_drained[bank], n + 1)
                nc.vector.scalar_tensor_tensor(out=xc[:, c % 2, h], in0=xc[:, c % 2, h], scalar=1.0,
                                               in1=xh[:, h], op0=ALU.add, op1=ALU.mult).then_inc(xc_ready, 1)

            def bc_less_hi(c):
                bank, n = front_use("X", c, 0)
                dve.wait_ge(bc_hi, c + 1)
                nc.vector.tensor_tensor(bc_rest[:], front[0:2 * BCR, bank], bc_parts[0:2 * BCR, c % 2],
                                        ALU.subtract).then_inc(front_drained[bank], 1)

            def bc_less_mid(c):
                dve.wait_ge(bc_mid, c + 1)
                nc.vector.tensor_tensor(bc_parts[0:BCR, c % 2], bc_rest[0:BCR], bc_parts[0:BCR, c % 2],
                                        ALU.subtract).then_inc(bc_ready, 1)

            def times_b(c, i):
                t = TILES * c + i
                m, h = divmod(i, HALVES)
                if i == 0 and c > 0:
                    dve.wait_ge(u_spread, SPREAD * c)
                if i < HALVES and c == 0:
                    for copied in u0_copied:
                        dve.wait_ge(copied, NQ // 2 * (i + 1))
                if h == 0:
                    dve.wait_ge(b_filled, QUADS * c + m + 1)
                if t >= RING:
                    dve.wait_ge(summed, t - RING + 1)
                tile = hbuf[:, t % RING]
                if c % ROW_CHUNKS == 0:
                    nc.vector.memset(tile[:, :, 0:1], 0.0)
                else:
                    nc.vector.tensor_copy(tile[:, :, 0], h_state[:, m, h])
                nc.vector.tensor_tensor(tile[:, :, 1:SEG], u_rep[:, c % 2, NQ * h:NQ * h + NQ],
                                        b_ps[:, m % 2].unsqueeze(1).broadcast_to([P, NQ, CH]),
                                        ALU.mult).then_inc(inp_ready, 1)

            def scan(c, i):
                t = TILES * c + i
                dve.wait_ge(inp_ready, t + 1)
                dve.wait_ge(decay_ready, t + 1)
                tile = hbuf[:, t % RING].rearrange("p s l -> p (s l)")
                nc.vector.tensor_tensor_scan(tile, decay[:, i % 2].rearrange("p s l -> p (s l)"), tile, 0.0,
                                             ALU.mult, ALU.add).then_inc(scanned, 1)

            def keep_state(c, i):
                t = TILES * c + i
                m, h = divmod(i, HALVES)
                dve.wait_ge(scanned, TILES * c + i + 1)
                nc.vector.tensor_copy(h_state[:, m, h], hbuf[:, t % RING, :, CH]).then_inc(h_ready, 1)

            def last_product():
                i = TILES - 1
                t = TILES * (NC - 1) + i
                bank, n = side_use("C", NC - 1, QUADS - 1)
                dve.wait_ge(side_drained[bank], n + 1)
                dve.wait_ge(scanned, t + 1)
                steps = hbuf[:, t % RING, :, 1:SEG]
                nc.vector.tensor_tensor(steps, steps, c_sb[:, QUADS - 1].unsqueeze(1).broadcast_to([P, NQ, CH]),
                                        ALU.mult).then_inc(last_prod_ready, 1)

            def gate_y(c, h):
                bank, n = side_use("G", c, h)
                dve.wait_ge(side_drained[bank], n + 1)
                dve.wait_ge(summed, TILES * (c + 1) - HALVES + h + 1)
                nc.vector.scalar_tensor_tensor(out=yg[:, h], in0=yg[:, h], scalar=1.0, in1=y_ps[:, h],
                                               op0=ALU.add, op1=ALU.mult).then_inc(y_gated, 1)

            nc.vector.memset(ones[:], 1.0)
            nc.vector.memset(bias_parts[:], 0.0)
            norm_stats(0)
            dve.wait_ge(cols_loaded, 16 * COLS)
            nc.vector.tensor_scalar(cb_col[:], cb_col[:], 0.5, None, ALU.mult)
            nc.vector.tensor_scalar(bg_col[:], bg_col[:], 0.5, None, ALU.mult).then_inc(cols_halved, 1)
            link(nc.vector.tensor_scalar(cw_col[:], cw_col[:], 0.5, None, ALU.mult))
            dve.wait_ge(ident_made, 1)
            for n in range(HALVES * TAPS):
                h, k = divmod(n, TAPS)
                ins = nc.vector.tensor_scalar(taps[:, n], ident[:], cw_col[:, h, k:k + 1], None, ALU.mult)
            ins.then_inc(taps_made, 1)
            norm_stats(1)
            dve.wait_ge(kern_loaded, 16)
            nc.vector.tensor_reduce(mx[:, 0:1], kern_nat, AX.X, ALU.max)
            link(nc.vector.tensor_reduce(mx[:, 1:2], kern_nat, AX.X, ALU.min))
            nc.vector.scalar_tensor_tensor(out=mx[:, 2:3], in0=mx[:, 1:2], scalar=-1.0, in1=mx[:, 0:1],
                                           op0=ALU.mult, op1=ALU.max).then_inc(absmax_own, 1)
            link(nc.vector.tensor_tensor(pick_f, ident[0:96, 0:32], ident[0:96, 32:64], ALU.add))
            link(nc.vector.tensor_tensor(pick_f, pick_f, ident[0:96, 64:96], ALU.add))
            nc.vector.tensor_copy(pick[:], pick_f.unsqueeze(2).broadcast_to([PARTS * BCR, BCR, Q]))
            nc.vector.tensor_copy(spread_q, ident[:].rearrange("p (q d) -> p q d", q=NQ).unsqueeze(2)
                                  .broadcast_to([P, NQ, NQ, Q]))
            link(nc.vector.tensor_tensor(sum_n4[:], ident[:, 0:Q], ident[:, Q:2 * Q], ALU.add))
            link(nc.vector.tensor_tensor(sum_n4[:], sum_n4[:], ident[:, 2 * Q:3 * Q], ALU.add))
            nc.vector.tensor_tensor(sum_n4[:], sum_n4[:], ident[:, 3 * Q:4 * Q], ALU.add).then_inc(picks_made, 1)
            dve.wait_ge(absmax_all, 1)
            s0, s_neg, s_lo, s_res, s_q, s_inv, ns_hi, ns_lo = (scale[:, i:i + 1] for i in range(8))
            link(nc.vector.tensor_scalar(s0, mx[:, 3:4], 1.0 / QMAX, None, ALU.mult))
            link(nc.vector.tensor_copy(scale_hi[:], s0))
            link(nc.vector.tensor_tensor(s_lo, s0, scale_hi[:], ALU.subtract))
            link(nc.vector.scalar_tensor_tensor(out=s_res, in0=scale_hi[:], scalar=-QMAX, in1=mx[:, 3:4],
                                                op0=ALU.mult, op1=ALU.add))
            link(nc.vector.scalar_tensor_tensor(out=s_res, in0=s_lo, scalar=-QMAX, in1=s_res,
                                                op0=ALU.mult, op1=ALU.add))
            link(nc.vector.scalar_tensor_tensor(out=s_q, in0=s_res, scalar=1.0 / QMAX, in1=s0,
                                                op0=ALU.mult, op1=ALU.add))
            link(nc.vector.reciprocal(s_inv, s_q))
            link(nc.vector.tensor_copy(scale_hi[:], s_q))
            link(nc.vector.tensor_tensor(ns_lo, scale_hi[:], s_q, ALU.subtract))
            link(nc.vector.tensor_scalar(ns_hi, scale_hi[:], -1.0, None, ALU.mult))
            link(nc.vector.tensor_scalar(s_neg, s_q, -1.0, None, ALU.mult))
            link(nc.vector.tensor_scalar(quant, kern_nat, s_inv, None, ALU.mult))
            link(nc.vector.tensor_scalar(q_hi, quant, SPLIT, None, ALU.add))
            link(nc.vector.tensor_scalar(q_hi, q_hi, -SPLIT, None, ALU.add))
            link(nc.vector.tensor_tensor(q_lo, quant, q_hi, ALU.subtract))
            link(nc.vector.scalar_tensor_tensor(out=q_res, in0=q_hi, scalar=ns_hi, in1=kern_nat,
                                                op0=ALU.mult, op1=ALU.add))
            link(nc.vector.scalar_tensor_tensor(out=q_res, in0=q_hi, scalar=ns_lo, in1=q_res,
                                                op0=ALU.mult, op1=ALU.add))
            link(nc.vector.scalar_tensor_tensor(out=q_res, in0=q_lo, scalar=s_neg, in1=q_res,
                                                op0=ALU.mult, op1=ALU.add))
            link(nc.vector.scalar_tensor_tensor(out=quant, in0=q_res, scalar=s_inv, in1=quant,
                                                op0=ALU.mult, op1=ALU.add))
            link(nc.vector.tensor_scalar(quant, quant, ROUND, None, ALU.add))
            link(nc.vector.tensor_scalar(quant, quant, -ROUND, -QMAX - 1.0, ALU.add, ALU.max))
            link(nc.vector.tensor_scalar(quant, quant, QMAX, s_q, ALU.min, ALU.mult))
            for h in range(HALVES):
                silu(0, h)
            dve.wait_ge(bca_transposed, 1)
            for part in range(PARTS):
                ins = nc.vector.tensor_copy(WbcT[:, :, part],
                                            b_ps[:, 1, 0:HALVES * BCR].rearrange("p (h r) -> p h r", h=HALVES))
            ins.then_inc(wbc_evicted, 1)
            nc.vector.tensor_copy(aT, b_ps[0:RANK, 1, 128:128 + D]).then_inc(aT_evicted, 1)
            dve.wait_ge(w_loaded, 16 * W_DMAS)
            link(nc.vector.tensor_tensor(brow, brow, brow2, ALU.add))
            link(nc.vector.tensor_copy(b_hi, brow))
            link(nc.vector.tensor_tensor(b_rest, brow, b_hi, ALU.subtract))
            link(nc.vector.tensor_copy(b_mid, b_rest))
            link(nc.vector.tensor_tensor(b_rest2, b_rest, b_mid, ALU.subtract))
            for part, src in enumerate((b_hi, b_mid, b_rest2)):
                r = slice(32 * part, 32 * part + 1)
                ins = nc.vector.tensor_copy(bias_parts[r], src[r].unsqueeze(1).broadcast_to([1, 2, D]))
            ins.then_inc(bias_made, 1)
            norm_stats(2)
            use = side_use("ab", 0, 0)
            wait_filled(dve, side_filled, use)
            nc.vector.tensor_tensor(Wff[:].rearrange("p h d -> p (h d)"), quant, side[:, use[0]],
                                    ALU.add).then_inc(side_drained[use[0]], 1)
            bc_less_hi(0)
            for h in range(HALVES):
                dve.wait_ge(sp_ready, h + 1)
                nc.vector.tensor_tensor(sp_lin[:, h], sp_lin[:, h], sp_log[:, h], ALU.add).then_inc(dt_ready, 1)
            for h in range(HALVES):
                dve.wait_ge(dt_ready, h + 1)
                nc.vector.tensor_tensor(sp_log[:, h], sp_lin[:, h], xc[:, 0, h], ALU.mult).then_inc(u_ready, 1)
            bc_less_mid(0)
            dve.wait_ge(a_exp, 1)
            nc.vector.tensor_scalar(a_col[:], a_col[:], -1.0, None, ALU.mult).then_inc(a_ready, 1)

            def copy_u0(k):
                dve.wait_ge(u0_filled, k + 1)
                nc.vector.tensor_copy(u_rep[:, 0, k], y_ps[:, 1]).then_inc(u0_copied[1], 1)

            copy_u0(1)
            copy_u0(3)
            times_b(0, 0)
            scan(0, 0)
            copy_u0(5)
            copy_u0(7)
            silu(1, 0)

            for c in range(NC):
                keeps = c % ROW_CHUNKS < ROW_CHUNKS - 1
                for i in range(TILES):
                    if TILES * c + i > 0:
                        scan(c, i)
                    if i + 1 < TILES:
                        times_b(c, i + 1)
                    if keeps:
                        keep_state(c, i)
                    if c > 0 and i == 2:
                        for h in range(HALVES):
                            gate_y(c - 1, h)
                    if i == 0 and c == 0:
                        silu(1, 1)
                    if i == 0 and c + 3 < NC:
                        norm_stats(c + 3)
                    if i == 4 and c + 1 < NC:
                        bc_less_hi(c + 1)
                    if i == 5 and c + 1 < NC:
                        bc_less_mid(c + 1)
                    if i in (2, 3) and c + 2 < NC:
                        silu(c + 2, i - 2)
                    if i + 1 == TILES and c + 1 < NC:
                        times_b(c + 1, 0)
            last_product()
            for h in range(HALVES):
                gate_y(NC - 1, h)

        @block.tensor
        def _(pe):
            def transposes(c):
                pe.wait_ge(xn_ready, c + 1)
                for h in range(HALVES):
                    use = front_use("T", c, h)
                    wait_free(pe, front_drained, use)
                    for tt in range(TT):
                        ins = nc.tensor.transpose(front[:, use[0], tt * P:(tt + 1) * P],
                                                  xin[:, c % 2, tt, h * P:(h + 1) * P], ident[:])
                    ins.then_inc(front_filled[use[0]], 1)

            def conv(c, h):
                use = front_use("V", c, h)
                wait_free(pe, front_drained, use)
                pe.wait_ge(pad_ready, c + 1)
                for j in range(TAPS):
                    ins = nc.tensor.matmul(front[:, use[0]], taps[:, h * TAPS + j],
                                           xnT[:, c % XRING, h, j:j + CH], start=(j == 0), stop=(j == TAPS - 1))
                ins.then_inc(front_filled[use[0]], 1)

            def delta(c, e):
                use = front_use("Z", c, e)
                pe.wait_ge(xc_ready, HALVES * (c + 1))
                wait_free(pe, front_drained, use)
                for h in range(HALVES):
                    ins = nc.tensor.matmul(front[:, use[0]], WdT[:, h, e * P:(e + 1) * P], xc[:, c % 2, h],
                                           start=(h == 0), stop=(h == HALVES - 1))
                ins.then_inc(front_filled[use[0]], 1)

            def proj_bc(c):
                use = front_use("X", c, 0)
                pe.wait_ge(xc_ready, HALVES * (c + 1))
                wait_free(pe, front_drained, use)
                for h in range(HALVES):
                    ins = nc.tensor.matmul(front[0:PARTS * BCR, use[0]], WbcT[:, h].rearrange("p a r -> p (a r)"),
                                           xc[:, c % 2, h], start=(h == 0), stop=(h == HALVES - 1))
                ins.then_inc(front_filled[use[0]], 1)

            def fill_b(c, m):
                if m == 0:
                    pe.wait_ge(bc_ready, c + 1)
                if c == 0 and m == 1:
                    pe.wait_ge(decay_ready, 1)
                if QUADS * c + m >= 2:
                    pe.wait_ge(inp_ready, TILES * c + HALVES * (m - 1))
                nc.tensor.matmul(b_ps[:, m % 2], pick[:, NQ * m:NQ * m + NQ].rearrange("r a q -> r (a q)"),
                                 bc_parts[:, c % 2], start=True, stop=True).then_inc(b_filled, 1)

            def fill_c(c, m):
                use = side_use("C", c, m)
                wait_free(pe, side_drained, use)
                if c == 0 and m == 1:
                    pe.wait_ge(decay_ready, 1)
                row = STATE + NQ * m
                nc.tensor.matmul(side[:, use[0]], pick[:, row:row + NQ].rearrange("r a q -> r (a q)"),
                                 bc_parts[:, c % 2], start=True, stop=True).then_inc(side_filled[use[0]], 1)

            def sum_states(c, i):
                t = TILES * c + i
                m, h = divmod(i, HALVES)
                if m == 0 and c > 0:
                    pe.wait_ge(y_gated, HALVES * (c - 1) + h + 1)
                if c == 0 and m == 0:
                    pe.wait_ge(u0_copied[h], BLOCKS // 2)
                if t + 1 < TILES * NC:
                    pe.wait_ge(prod_ready, t + 1)
                else:
                    pe.wait_ge(last_prod_ready, 1)
                for q in range(NQ):
                    ins = nc.tensor.matmul(y_ps[Q * q:Q * q + Q, h], sum_n4[:], hbuf[:, t % RING, q, 1:SEG],
                                           start=(m == 0), stop=(m == QUADS - 1))
                ins.then_inc(summed, 1)

            def gate(c, e):
                use = side_use("G", c, e)
                wait_free(pe, side_drained, use)
                for h in range(HALVES):
                    ins = nc.tensor.matmul(side[:, use[0]], WgT[:, h, e * P:(e + 1) * P],
                                           xnT[:, c % XRING, h, PAD:PAD + CH],
                                           start=(h == 0), stop=(h == HALVES - 1))
                ins.then_inc(side_filled[use[0]], 1)

            def out_product_x(c, j):
                use = side_use("E", c, j)
                wait_free(pe, side_drained, use)
                nc.tensor.matmul(side[:, use[0]], ones[:], bias_parts[:].rearrange("p t d -> p (t d)"),
                                 start=True, stop=False)
                for tt in range(2):
                    tok = (2 * j + tt) * P
                    for h in range(HALVES):
                        nc.tensor.matmul(side[:, use[0], tt * D:(tt + 1) * D],
                                         xnT[:, c % XRING, h, PAD + tok:PAD + tok + P], Wff[:, h],
                                         start=False, stop=False)
                pe.wait_ge(xres_loaded[j], 16 * (c + 1))
                nc.tensor.matmul(side[:, use[0]], ident[:], xres[:, j].rearrange("p t d -> p (t d)"),
                                 start=False, stop=False)

            def out_product_y(c, j):
                use = side_use("E", c, j)
                pe.wait_ge(y_gated, HALVES * (c + 1))
                for tt in range(2):
                    tok = (2 * j + tt) * P
                    for h in range(HALVES):
                        ins = nc.tensor.matmul(side[:, use[0], tt * D:(tt + 1) * D], yg[:, h, tok:tok + P],
                                               WoT[:, h], start=False, stop=(tt == 1 and h == HALVES - 1))
                ins.then_inc(side_filled[use[0]], 1)

            def transpose_w(dst, nat):
                for h in range(HALVES):
                    for e in range(HALVES):
                        ins = nc.tensor.transpose(dst[:, h * D + e * P:h * D + (e + 1) * P],
                                                  nat[:, e, h * P:(h + 1) * P], ident[:])
                return ins

            pe.wait_ge(ident_made, 1)
            transposes(0)
            pe.wait_ge(wd_loaded, 16)
            transpose_w(y_ps[:, 0], wd_nat).then_inc(wd_transposed, 1)
            pe.wait_ge(taps_made, 1)
            for h in range(HALVES):
                conv(0, h)
            transposes(1)
            pe.wait_ge(w_loaded, 16 * W_DMAS)
            for h in range(HALVES):
                nc.tensor.transpose(b_ps[:, 1, h * BCR:(h + 1) * BCR], wbc_nat[:, h * P:(h + 1) * P],
                                    ident[0:BCR, 0:BCR])
            for h in range(HALVES):
                ins = nc.tensor.transpose(b_ps[0:RANK, 1, 128 + h * P:128 + (h + 1) * P], a_nat[:, h], ident[:])
            ins.then_inc(bca_transposed, 1)
            transpose_w(y_ps[:, 1], wg_nat)
            transpose_w(b_ps[:, 0], wo_nat).then_inc(w_transposed, 1)
            pe.wait_ge(w_evicted, 1)
            for e in range(HALVES):
                delta(0, e)
            pe.wait_ge(wbc_evicted, 1)
            proj_bc(0)
            pe.wait_ge(aT_evicted, 1)
            use = side_use("ab", 0, 0)
            for h in range(HALVES):
                ins = nc.tensor.matmul(side[:, use[0], h * D:(h + 1) * D], aT[:, h * P:(h + 1) * P], b_nat,
                                       start=True, stop=True)
            ins.then_inc(side_filled[use[0]], 1)
            conv(1, 0)
            pe.wait_ge(w_evicted, 3)
            pe.wait_ge(picks_made, 1)
            for k in range(BLOCKS):
                h, q = divmod(k, NQ)
                pe.wait_ge(u_ready, h + 1)
                if k >= 2:
                    pe.wait_ge(u0_copied[k % 2], k // 2)
                nc.tensor.matmul(y_ps[:, k % 2], spread_q[:, q].rearrange("p n d -> p (n d)"),
                                 sp_log[:, h], start=True, stop=True).then_inc(u0_filled, 1)
                if k == NQ - 1:
                    fill_b(0, 0)
                    fill_c(0, 0)
                    pe.wait_ge(side_drained[0], 1)
                    for q in range(NQ):
                        if q >= 2:
                            pe.wait_ge(dt0_used, q - 1)
                        nc.tensor.matmul(dt0_banks[q % 2], spread_q[:, q].rearrange("p n d -> p (n d)"),
                                         sp_lin[:, 0], start=True, stop=True).then_inc(dt0_filled, 1)
            conv(1, 1)

            for c in range(NC):
                for i in range(TILES):
                    t = TILES * c + i
                    if i % HALVES == 0 and t + 2 < TILES * NC:
                        m = i // HALVES + 1
                        fill_b(c + m // QUADS, m % QUADS)
                    for kind, chunk, m in side_slot(c, i):
                        if kind == "C":
                            fill_c(chunk, m)
                        if kind == "G":
                            gate(chunk, m)
                    if t >= 3:
                        sum_states((t - 3) // TILES, (t - 3) % TILES)
                    for kind, k in FRONT_SLOTS.get(i, []):
                        if kind == "Z" and c + 2 < NC:
                            delta(c + 2, k)
                        if kind == "T" and k == 0 and c + 2 < NC:
                            transposes(c + 2)
                        if kind == "X" and c + 1 < NC:
                            proj_bc(c + 1)
                        if kind == "V" and c + 2 < NC:
                            conv(c + 2, k)
                    if t == 0:
                        for e in range(HALVES):
                            delta(1, e)
                    for kind, chunk, j in side_slot(c, i):
                        if kind == "E":
                            if chunk == 0 and j == 0:
                                pe.wait_ge(bias_made, 1)
                            out_product_x(chunk, j)
                            if chunk < c:
                                out_product_y(chunk, j)
            for i in range(TILES - 3, TILES):
                sum_states(NC - 1, i)
            out_product_x(NC - 1, 1)
            for j in range(OUTS):
                out_product_y(NC - 1, j)


_INS = ['L0_attn_x', 'L0_attn_conv_w', 'L0_attn_conv_b', 'L0_attn_Wd', 'L0_attn_bd', 'L0_attn_Wb', 'L0_attn_Wc',
        'L0_attn_log_a', 'L0_attn_Wg', 'L0_attn_bg', 'L0_attn_Wo', 'L0_attn_bo', 'L0_ffn_kernel', 'L0_ffn_bias',
        'L0_ffn_a', 'L0_ffn_b']


def kernel(**inputs):
    import numpy as _np
    import concourse.bacc as _bacc
    from concourse import mybir as _mybir
    from concourse.bass_utils import run_bass_kernel_spmd as _run

    nc = _bacc.Bacc("TRN2", target_bir_lowering=False, num_devices=1)
    arrays, args = {}, []
    for name in _INS:
        v = _np.ascontiguousarray(inputs[name])
        arrays[f"in_{name}_dram"] = v
        args.append(nc.dram_tensor(f"in_{name}_dram", v.shape, _mybir.dt.from_np(v.dtype), kind="ExternalInput").ap())
    shape = inputs['L0_attn_x'].shape
    args.append(nc.dram_tensor("out_0_dram", shape, _mybir.dt.float32, kind="ExternalOutput").ap())
    build_layer(nc, *args)
    r = _run(nc, [arrays], core_ids=[0])
    return r.results[0]["out_0_dram"]
```
